# Optimizing a Trainium2 kernel written in Bass

```python
import numpy as np
import jax
import jax.numpy as jnp

def _softmax(x, axis=-1):
    return jax.nn.softmax(x, axis=axis)

def _gelu(x):
    return jax.nn.gelu(x, approximate=True)

def _silu(x):
    return jax.nn.silu(x)

def _sigmoid(x):
    return jax.nn.sigmoid(x)

def _layernorm(x, axis=-1, eps=1e-05):
    m = jnp.mean(x, axis=axis, keepdims=True)
    v = jnp.var(x, axis=axis, keepdims=True)
    return (x - m) / jnp.sqrt(v + eps)

def _scatter_add(tgt, idx, src, axis=0):
    return tgt.at[idx].add(src)

def _segment_sum(src, seg, n):
    return jax.ops.segment_sum(src, seg, n)
kernel_name = 'mk_conv_seq_d2_conv_nchw64_r2_2a6a9c'

def setup_inputs(seed: int=0):
    np.random.seed(seed)
    _w = jnp.asarray

    def _rec_inputs():
        import jax
        import jax.numpy as jnp
        _gk = jax.random.key(seed)
        x = -0.000125 + 0.9999 * jax.random.normal(jax.random.fold_in(_gk, 1), (8, 32, 128, 128), jnp.float32)
        return x
    x = _rec_inputs()

    def _L0_conv_setup():
        import jax, jax.numpy as jnp
        import numpy as np
        K = 3
        D = 1
        G = 8
        BN_EPS = 1e-05
        key = jax.random.key(seed)
        ks = jax.random.split(key, 8)
        N, C, H, W = (8, 32, 128, 128)
        k2 = K * K
        x = jax.random.normal(ks[0], (N, C, H, W), jnp.float32)
        conv_w = jax.random.normal(ks[1], (G * k2, C), jnp.float32) * (2.0 / C) ** 0.5
        bn_gamma = jnp.ones((G * k2,), jnp.float32)
        bn_beta = jnp.zeros((G * k2,), jnp.float32)
        bn_mean = jax.random.normal(ks[2], (G * k2,), jnp.float32) * 0.01
        bn_var = jax.random.uniform(ks[3], (G * k2,), jnp.float32, 0.5, 1.5)
        lamb_l = jax.random.normal(ks[4], (C,), jnp.float32) * 0.1
        lamb_h = jax.random.normal(ks[5], (C,), jnp.float32) * 0.1
        inside_all = jax.random.normal(ks[6], (C, 1, 1), jnp.float32) * 0.1
        return {'x': x, 'conv_w': conv_w, 'bn_gamma': bn_gamma, 'bn_beta': bn_beta, 'bn_mean': bn_mean, 'bn_var': bn_var, 'lamb_l': lamb_l, 'lamb_h': lamb_h, 'inside_all': inside_all}
    _L0_conv_all = _L0_conv_setup()
    _L0_conv_in = {k: v for k, v in _L0_conv_all.items() if k in ('conv_w', 'bn_gamma', 'bn_beta', 'bn_mean', 'bn_var', 'lamb_l', 'lamb_h', 'inside_all')}
    del _L0_conv_all

    def _L1_conv_setup():
        import jax, jax.numpy as jnp
        import numpy as np
        from jax import lax
        CUTOFF = 0.25
        SIGMA = 1.0
        RADIUS = 4

        def _gauss_kernel(sigma=SIGMA, radius=RADIUS):
            x = np.arange(-radius, radius + 1, dtype=np.float32)
            k = np.exp(-0.5 * (x / sigma) ** 2)
            return jnp.asarray(k / k.sum())

        def _blur_axis(x, axis, kernel):
            r = (kernel.shape[0] - 1) // 2
            pad = [(0, 0)] * x.ndim
            pad[axis] = (r, r)
            xp = jnp.pad(x, pad, mode='edge')
            out = jnp.zeros_like(x)
            for i in range(kernel.shape[0]):
                out = out + kernel[i] * lax.slice_in_dim(xp, i, i + x.shape[axis], axis=axis)
            return out

        def gaussian_smoothing_4d(x):
            k = _gauss_kernel().astype(x.dtype)
            for ax in range(4):
                x = _blur_axis(x, ax, k)
            return x

        def dht_2d(x):
            return (jnp.fft.fftn(x, axes=(2, 3)).real - jnp.fft.fftn(jnp.flip(x, axis=(2, 3)), axes=(2, 3)).imag).astype(x.dtype)

        def _neg_k(a):
            return jnp.roll(jnp.flip(a, axis=(-2, -1)), shift=(1, 1), axis=(-2, -1))

        def compl_mul2d(x1, x2):
            x1n, x2n = (_neg_k(x1), _neg_k(x2))
            e = lambda a, b: jnp.einsum('bixy,ioxy->boxy', a, b)
            return 0.5 * (e(x1, x2) - e(x1n, x2n) + e(x1, x2n) + e(x1n, x2))
        key = jax.random.key(seed)
        k1, k2 = jax.random.split(key)
        B, Cin, Cout, H, W, M1, M2 = (16, 32, 32, 64, 64, 20, 20)
        x = jax.random.normal(k1, (B, Cin, H, W), dtype=jnp.float32)
        scale = 1.0 / (Cin * Cout)
        w1 = scale * jax.random.uniform(k2, (Cin, Cout, M1, M2), dtype=jnp.float32)
        return {'x': x, 'w1': w1}
    _L1_conv_all = _L1_conv_setup()
    _L1_conv_in = {k: v for k, v in _L1_conv_all.items() if k in ('w1',)}
    del _L1_conv_all
    return {'x': x, 'L0_conv_conv_w': _L0_conv_in['conv_w'], 'L0_conv_bn_gamma': _L0_conv_in['bn_gamma'], 'L0_conv_bn_beta': _L0_conv_in['bn_beta'], 'L0_conv_bn_mean': _L0_conv_in['bn_mean'], 'L0_conv_bn_var': _L0_conv_in['bn_var'], 'L0_conv_lamb_l': _L0_conv_in['lamb_l'], 'L0_conv_lamb_h': _L0_conv_in['lamb_h'], 'L0_conv_inside_all': _L0_conv_in['inside_all'], 'L1_conv_w1': _L1_conv_in['w1']}

def reference(x, L0_conv_conv_w, L0_conv_bn_gamma, L0_conv_bn_beta, L0_conv_bn_mean, L0_conv_bn_var, L0_conv_lamb_l, L0_conv_lamb_h, L0_conv_inside_all, L1_conv_w1):
    import jax
    import jax.numpy as jnp

    def _L0_conv_ref(x, conv_w, bn_gamma, bn_beta, bn_mean, bn_var, lamb_l, lamb_h, inside_all):
        import jax, jax.numpy as jnp
        import numpy as np
        K = 3
        D = 1
        G = 8
        BN_EPS = 1e-05
        N, C, H, W = x.shape
        k2 = K * K
        pooled = x.mean(axis=(2, 3))
        lf = pooled @ conv_w.T
        lf = (lf - bn_mean) * (bn_gamma / jnp.sqrt(bn_var + BN_EPS)) + bn_beta
        lf = jnp.tanh(lf).reshape(N, G, 1, k2, 1)
        p = D * (K - 1) // 2
        xp = jnp.pad(x, ((0, 0), (0, 0), (p, p), (p, p)), mode='reflect')
        patches = jnp.stack([xp[:, :, i * D:i * D + H, j * D:j * D + W] for i in range(K) for j in range(K)], axis=2)
        xu = patches.reshape(N, G, C // G, k2, H * W)
        low_part = jnp.sum(xu * lf, axis=3).reshape(N, C, H, W)
        gap = x.mean(axis=(2, 3), keepdims=True)
        out_low = (low_part * (inside_all + 1.0) - inside_all * gap) * lamb_l[None, :, None, None]
        out_high = x * (lamb_h[None, :, None, None] + 1.0)
        return out_low + out_high

    def _L1_conv_ref(x, w1):
        import jax, jax.numpy as jnp
        import numpy as np
        from jax import lax
        CUTOFF = 0.25
        SIGMA = 1.0
        RADIUS = 4

        def _gauss_kernel(sigma=SIGMA, radius=RADIUS):
            x = np.arange(-radius, radius + 1, dtype=np.float32)
            k = np.exp(-0.5 * (x / sigma) ** 2)
            return jnp.asarray(k / k.sum())

        def _blur_axis(x, axis, kernel):
            r = (kernel.shape[0] - 1) // 2
            pad = [(0, 0)] * x.ndim
            pad[axis] = (r, r)
            xp = jnp.pad(x, pad, mode='edge')
            out = jnp.zeros_like(x)
            for i in range(kernel.shape[0]):
                out = out + kernel[i] * lax.slice_in_dim(xp, i, i + x.shape[axis], axis=axis)
            return out

        def gaussian_smoothing_4d(x):
            k = _gauss_kernel().astype(x.dtype)
            for ax in range(4):
                x = _blur_axis(x, ax, k)
            return x

        def dht_2d(x):
            return (jnp.fft.fftn(x, axes=(2, 3)).real - jnp.fft.fftn(jnp.flip(x, axis=(2, 3)), axes=(2, 3)).imag).astype(x.dtype)

        def _neg_k(a):
            return jnp.roll(jnp.flip(a, axis=(-2, -1)), shift=(1, 1), axis=(-2, -1))

        def compl_mul2d(x1, x2):
            x1n, x2n = (_neg_k(x1), _neg_k(x2))
            e = lambda a, b: jnp.einsum('bixy,ioxy->boxy', a, b)
            return 0.5 * (e(x1, x2) - e(x1n, x2n) + e(x1, x2n) + e(x1n, x2))
        B, _, H, W = x.shape
        Cout, M1, M2 = (w1.shape[1], w1.shape[2], w1.shape[3])
        x_ht = dht_2d(x)
        out_ht = jnp.zeros((B, Cout, H, W), dtype=x.dtype)
        out_ht = out_ht.at[:, :, :M1, :M2].set(compl_mul2d(x_ht[:, :, :M1, :M2], w1))
        y = dht_2d(out_ht) / (H * W)
        y = gaussian_smoothing_4d(y)
        freqs = jnp.fft.fftfreq(W)
        mask = (jnp.abs(freqs) <= CUTOFF).astype(y.dtype)
        return y * mask

    def _gn(v, G=32, eps=1e-05):
        B_, C_, H_, W_ = v.shape
        g = v.reshape(B_, G, C_ // G, H_, W_)
        m = jnp.mean(g, axis=(2, 3, 4), keepdims=True)
        s = jnp.var(g, axis=(2, 3, 4), keepdims=True)
        return ((g - m) / jnp.sqrt(s + eps)).reshape(v.shape)

    def _ln_c(v, eps=1e-06):
        m = jnp.mean(v, axis=1, keepdims=True)
        s = jnp.var(v, axis=1, keepdims=True)
        return (v - m) / jnp.sqrt(s + eps)

    def _ln_t(v, eps=1e-05):
        m = jnp.mean(v, axis=-1, keepdims=True)
        s = jnp.var(v, axis=-1, keepdims=True)
        return (v - m) / jnp.sqrt(s + eps)

    def _to_tokens(v):
        B_, C_, H_, W_ = v.shape
        return v.reshape(B_, C_, H_ * W_).transpose(0, 2, 1)

    def _from_tokens(t, like):
        B_, C_, H_, W_ = like.shape
        return t.transpose(0, 2, 1).reshape(B_, C_, H_, W_)
    x = _L0_conv_ref(x, L0_conv_conv_w, L0_conv_bn_gamma, L0_conv_bn_beta, L0_conv_bn_mean, L0_conv_bn_var, L0_conv_lamb_l, L0_conv_lamb_h, L0_conv_inside_all)
    x = _L1_conv_ref(x, L1_conv_w1)
    return x

_drawn_inputs = setup_inputs


def setup_inputs(seed=0):
    import zlib

    import numpy as np

    out = dict(_drawn_inputs(seed))
    spreads = {'L0_conv_bn_gamma': (1.0, 0.6), 'L0_conv_bn_beta': (0.0, 0.443)}
    factors = {'L0_conv_conv_w': 73.255,
     'L0_conv_bn_mean': 138.973,
     'L0_conv_bn_var': 200.0,
     'L0_conv_inside_all': 8.0}
    for name, (base, spread) in spreads.items():
        noise = np.random.default_rng([zlib.crc32(name.encode()), seed]).standard_normal(out[name].shape)
        drawn = base * np.exp(spread * noise) if base else spread * noise
        out[name] = jnp.asarray(drawn.astype(out[name].dtype))
    for name, factor in factors.items():
        out[name] = (out[name] * factor).astype(out[name].dtype)
    return out
```

```python
from contextlib import ExitStack

import numpy as np

import concourse.bass as bass
from concourse import mybir

N, C, H = 8, 32, 128
MODES = 20
GROUPS, TAPS = 8, 9
J, Q, S = 4, 3, 2
SQ = S * Q
NP = SQ * 2 * J + 2 * J
NU = 2 * MODES + 4
NEDGE = 2 * (S * MODES + 1)
NDATA = SQ * NU + 2 * NEDGE
KT = TAPS + 1
KROWS = KT * J
PLANE = SQ * MODES
ND, NA, NB = 2 * PLANE, 3 * SQ * 8, 4 * PLANE
NTERM = 9
HALF = 33
NW = 2 * HALF
NF = 21 * 2
TRIPLES = 11
BPAD = 32

O_LT, O_RU = 0, 4 * NP
O_RE = O_RU + S * 2 * NU
O_BAS = O_RE + NEDGE
O_BT = O_BAS + 3 * PLANE
O_BC = O_BT + N * N
O_TW = O_BC + Q * C
O_LH = O_TW + NW
NC128 = O_LH + 3 * H
O_TAB = 0
O_MA = ND + NA + NB
O_MB, O_MC = O_MA + H, O_MA + 2 * H
O_PICK = O_MA + 3 * H
NC40 = O_PICK + GROUPS * TAPS
P_L, P_H, P_IN = 0, C, 2 * C
P_GAMMA = 3 * C
P_BETA, P_MEAN, P_VAR = P_GAMMA + GROUPS, P_GAMMA + 2 * GROUPS, P_GAMMA + 3 * GROUPS
NPAR = P_GAMMA + 4 * GROUPS


def frequency(s, j, q):
    a = min(Q * j + q, MODES // 2)
    return a if s == 0 else (MODES - a) % MODES


def column(s, b):
    return b if s == 0 else (MODES - b) % MODES


def blur_matrix(n):
    k = np.exp(-0.5 * np.arange(-4, 5, dtype=np.float32) ** 2)
    k = (k / k.sum()).astype(np.float64)
    m = np.zeros((n, n))
    for o in range(n):
        for i in range(9):
            m[o, min(max(o + i - 4, 0), n - 1)] += k[i]
    return m


def constants():
    th = 2 * np.pi / H
    h = np.arange(H)
    e1, e2 = np.zeros(H), np.zeros(H)
    e1[1], e1[H - 1] = 1, -1
    e2[H - 2], e2[0] = 1, -1
    lt = np.zeros((H, NP))
    ru = np.zeros((H, S, 2, NU))
    re = np.zeros((H, NEDGE))
    basis = np.zeros((3, S, Q, MODES))
    for s in range(S):
        for q in range(Q):
            for j in range(J):
                a = frequency(s, j, q)
                lt[:, ((s * Q + q) * 2) * J + j] = np.cos(th * a * h)
                lt[:, ((s * Q + q) * 2 + 1) * J + j] = np.sin(th * a * h)
        for b in range(MODES):
            bb = column(s, b)
            c, sn = np.cos(th * bb * h), np.sin(th * bb * h)
            ru[:, s, 0, b], ru[:, s, 0, MODES + b] = c, sn
            ru[:, s, 1, b], ru[:, s, 1, MODES + b] = -sn, c
            re[:, s * MODES + b], re[:, NEDGE // 2 + s * MODES + b] = c, sn
            basis[:, s, :, b] = np.array([1, np.cos(th * bb), np.sin(th * bb)])[:, None]
        ru[:, s, 0, 2 * MODES], ru[:, s, 0, 2 * MODES + 1] = e1, e2
        ru[:, s, 1, 2 * MODES + 2], ru[:, s, 1, 2 * MODES + 3] = e1, e2
    lt[:, NP - 2 * J:NP - J], lt[:, NP - J:] = e1[:, None], e2[:, None]
    re[:, NEDGE // 2 - 1], re[:, NEDGE - 1] = e1, e2

    d = np.zeros((KT, J, 2, S, Q, MODES))
    e = np.zeros((KT, J, 4, S, Q, MODES))
    f = np.zeros((KT, J, 3, S, Q, 8))
    for j in range(J):
        for s in range(S):
            for q in range(Q):
                a = frequency(s, j, q)
                ea = np.exp(1j * th * a)
                for b in range(MODES):
                    bb = column(s, b)
                    eb = np.exp(1j * th * bb)
                    g = 1 - 1j * np.conj(ea) * np.conj(eb)
                    for di in (-1, 0, 1):
                        for dj in (-1, 0, 1):
                            t = (di + 1) * 3 + dj + 1
                            k = g * ea ** di * eb ** dj
                            d[t, j, 0, s, q, b], d[t, j, 1, s, q, b] = k.real, k.imag
                            if di:
                                r = 0 if di < 0 else 2
                                z = g * (1 if di < 0 else ea) * eb ** dj
                                e[t, j, r, s, q, b], e[t, j, r + 1, s, q, b] = z.real, z.imag
                    if a == 0 and bb == 0:
                        d[TAPS, j, 0, s, q, b] = 1
                for di in (-1, 0, 1):
                    for dj in (-1, 1):
                        t, r = (di + 1) * 3 + dj + 1, (0 if dj < 0 else 1)
                        parts = [(r, ea ** di), (2 + r, -1j * ea ** di)]
                        if di:
                            parts.append((4 + (0 if di < 0 else 2) + r, 1 if di < 0 else ea))
                        for k, z in parts:
                            m = ([z, -1j * z * np.conj(ea), -z * np.conj(ea)] if dj < 0
                                 else [-1j * np.conj(ea) * z, z, 1j * z])
                            f[t, j, :, s, q, k] = np.real(m)
    table = np.concatenate([d.reshape(KROWS, ND), f.reshape(KROWS, NA), e.reshape(KROWS, NB)], 1)

    kept = np.concatenate([np.arange(HALF), np.arange(H - HALF, H)])
    tw = np.zeros((2, 2, BPAD, H))
    for b in range(MODES):
        tw[0, 0, b], tw[0, 1, b] = np.cos(th * h * b), -np.sin(th * h * (b + 1))
        tw[1, 0, b], tw[1, 1, b] = -np.sin(th * h * b), -np.cos(th * h * (b + 1))
    rows = blur_matrix(H)
    tw = (tw.reshape(128, H) @ rows.T)[:, kept] * (0.5 / (H * H))
    tw[:, HALF] = 0
    lh = np.zeros((3, 128, H))
    for s in range(3):
        for a in range(MODES + 1):
            lh[s, s * NF + 2 * a] = rows @ np.cos(th * h * a)
            lh[s, s * NF + 2 * a + 1] = rows @ np.sin(th * h * a)

    wide = np.zeros((128, NC128), np.float32)
    pair = np.zeros((2, H // 2, 2, 2, NP))
    for i in range(2):
        pair[i, :, :, i] = lt.reshape(H // 2, 2, NP)
    wide[:, O_LT:O_RU] = pair.reshape(H, 4 * NP)
    wide[:, O_RU:O_RE] = ru.reshape(H, -1)
    wide[:, O_RE:O_BAS] = re
    wide[:, O_BAS:O_BT] = basis.reshape(1, -1)
    wide[:, O_BT:O_BC] = blur_matrix(N).T.reshape(1, -1)
    wide[:Q * C, O_BC:O_TW] = np.kron(np.eye(Q), blur_matrix(C).T)
    wide[:, O_TW:O_LH] = tw
    wide[:, O_LH:] = lh.transpose(1, 0, 2).reshape(128, -1)

    t, own = np.arange(KROWS) // J, np.kron(np.arange(KROWS) % J, 1)[:, None] == (np.arange(128) // C)[None]
    narrow = np.zeros((KROWS, NC40), np.float32)
    narrow[:, O_TAB:O_MA] = table
    narrow[:, O_MA:O_MB] = own * (t < TAPS)[:, None]
    narrow[:, O_MB:O_MC] = own * (t == TAPS // 2)[:, None]
    narrow[:, O_MC:O_PICK] = -1.0 * own * (t == TAPS)[:, None]
    narrow[:, O_PICK:] = np.tile(t[:, None] == np.arange(TAPS)[None], (1, GROUPS))
    return wide, narrow


def hartley_conv_kernel(nc, x, wide, narrow, params, conv_wt, mix_w, out):
    fp32 = mybir.dt.float32
    ALU = mybir.AluOpType
    ACT = mybir.ActivationFunctionType
    AX = mybir.AxisListType
    HC = C // 2
    G1 = 8
    NG1 = C // G1

    def view(ap, *dims):
        return bass.AP(tensor=ap.tensor, offset=ap.offset, ap=[ap.ap[0], *[list(d) for d in dims]])

    def from_(n, least):
        return not isinstance(n, int) or n >= least

    ctx = ExitStack()
    with ctx:
        def sb(name, shape):
            return ctx.enter_context(nc.sbuf_tensor(name, shape, fp32))

        def sem(name):
            return ctx.enter_context(nc.semaphore(name))

        x_ring = sb("x_ring", [H, 2, C // 2, 2 * H])
        k_wide = sb("k_wide", [128, NC128])
        k_narrow = sb("k_narrow", [KROWS, NC40])
        par = sb("par", [KROWS, NPAR])
        conv_sb = sb("conv_sb", [C, GROUPS * TAPS])
        w_sb = sb("w_sb", [128, S, Q * MODES, C])
        y_sb = sb("y_sb", [H, NP, C])
        data = sb("data", [128, 2, NDATA])
        pooled = sb("pooled", [C, 1])
        bn = sb("bn", [KROWS, 2, GROUPS])
        gain = sb("gain", [KROWS, 3, C])
        pick = sb("pick", [KROWS, GROUPS, TAPS])
        kb_mul = sb("kb_mul", [KROWS, 128])
        kb_add = sb("kb_add", [KROWS, 128])
        kb_tmp = sb("kb_tmp", [KROWS, 128])
        kb = sb("kb", [KROWS, 128])
        lf_all = sb("lf_all", [KROWS, GROUPS * TAPS])
        lf = sb("lf", [KROWS, GROUPS])
        lf_bn = sb("lf_bn", [KROWS, GROUPS])
        lf_tanh = sb("lf_tanh", [KROWS, GROUPS])
        prod_a = sb("prod_a", [128, 3 * SQ, 8])
        coef_a = sb("coef_a", [128, 3 * SQ])
        terms = sb("terms", [128, NTERM, PLANE])
        xht = sb("xht", [128, 2, PLANE])
        spread = sb("spread", [128, N, PLANE])
        acc = sb("acc", [128, N, PLANE])
        mixin = sb("mixin", [128, Q * MODES, J, 3, N])
        mixed = sb("mixed", [Q * C, N, S * J, BPAD])
        mixed_n = sb("mixed_n", [Q * C, 2, S * J, 4 * BPAD])
        modes = sb("modes", [128, 2, C + 1, NF])
        cols = sb("cols", [3 * NF, 2, TRIPLES, NW])
        rows = sb("rows", [H, 2, C, H])
        ps = ctx.enter_context(nc.psum_tensor("ps", [128, 8, 512], fp32))

        consts_in, params_in, narrow_in, rest_in, weights_in = map(
            sem, ("consts_in", "params_in", "narrow_in", "rest_in", "weights_in"))
        x_in = [sem(f"x_in{i}") for i in range(4)]
        s1_done, y_out, s2_done, pool_done, data_out = map(
            sem, ("s1_done", "y_out", "s2_done", "pool_done", "data_out"))
        setup, root_done, lf_done, k_step, bn_done, tanh_done, kb_done = map(
            sem, ("setup", "root_done", "lf_done", "k_step", "bn_done", "tanh_done", "kb_done"))
        coef_done, coef_used, f_step, xht_done, spread_done, acc_done = map(
            sem, ("coef_done", "coef_used", "f_step", "xht_done", "spread_done", "acc_done"))
        zeroed, eo_dve, eo_pool, mix_done, mixed_act, mixed_dve = map(
            sem, ("zeroed", "eo_dve", "eo_pool", "mix_done", "mixed_act", "mixed_dve"))
        pick_done, tr_done, modes_act, modes_dve, t_done, cols_act, cols_dve = map(
            sem, ("pick_done", "tr_done", "modes_act", "modes_dve", "t_done", "cols_act", "cols_dve"))
        f_done, rows_act, rows_dve = map(sem, ("f_done", "rows_act", "rows_dve"))
        out_done = [sem(f"out_done{i}") for i in range(2)]

        B_DATA, B_LF, B_COEF = 4, 5, 6
        B_TR, B_T, B_F = 3, 5, (7, 0, 1)
        K_LINKS, F_LINKS = 3, 3

        wide_row = k_wide[:, 0:1]

        def const(offset, *dims, rows_=128):
            return view(k_wide[0:rows_, offset:offset + 1], *dims)

        block = ctx.enter_context(nc.Block())

        CHUNKS = [(s, t, (6 if t == 0 else (5 if s < 2 else 4))) for s in range(3) for t in (0, 6)]

        @block.sync
        def _(sp):
            pairs = x.rearrange("n (k s) (p r) w -> n (s p) k (r w)", s=2, r=2)

            def load(n, u):
                for half in range(2):
                    if from_(n, 2):
                        sp.wait_ge(s1_done, (n - 2) * NG1 + (half + 1) * NG1 // 2)
                    sp.dma_start(x_ring[:, u, half * HC // 2:(half + 1) * HC // 2, :],
                                 pairs[n, :, half * HC // 2:(half + 1) * HC // 2, :]
                                 ).then_inc(x_in[2 * u + half], 16)

            sp.dma_start(k_wide[:, 0:O_BAS], wide[:, 0:O_BAS]).then_inc(consts_in, 16)
            load(0, 0)
            sp.dma_start(par[:, :], params).then_inc(params_in, 16)
            sp.dma_start(conv_sb[:, :], conv_wt).then_inc(params_in, 16)
            sp.dma_start(k_narrow[:, :], narrow).then_inc(narrow_in, 16)
            sp.dma_start(k_wide[:, O_BAS:], wide[:, O_BAS:]).then_inc(rest_in, 16)
            load(1, 1)
            for n in range(2, N):
                load(n, n % 2)
            sp.dma_start(w_sb[:, :, :, :], mix_w).then_inc(weights_in, 16)

            def store(n, u):
                sp.wait_ge(rows_act, n * 3 + 3)
                sp.wait_ge(rows_dve, n * 3 + 3)
                dst = out[bass.ds(n, 1), :, :, :] if not isinstance(n, int) else out[n:n + 1, :, :, :]
                sp.dma_start(dst.rearrange("a c h w -> h (a c) w"), rows[:, u, :, :]).then_inc(out_done[u], 16)

            with sp.Fori(0, N // 2) as it:
                for u in range(2):
                    store(it * 2 + u, u)
            for u in range(2):
                sp.wait_ge(out_done[u], 16 * (N // 2))

        @block.tensor
        def _(pe):
            def stage1(n, it, u):
                for g in range(NG1):
                    if g % 2 == 0:
                        pe.wait_ge(x_in[2 * u + g // 2], it * 16 + 16)
                    if from_(n, 1):
                        pe.wait_ge(y_out, (n - 1) * NG1 + g + 1)
                    for i in range(G1 // 2):
                        for r in range(2):
                            last = nc.tensor.matmul(ps[:, g, 2 * i * NP:2 * (i + 1) * NP],
                                                    x_ring[:, u, g * G1 // 2 + i, r * H:(r + 1) * H],
                                                    const(O_LT + r * 2 * NP, (1, 2 * NP)),
                                                    start=(r == 0), stop=(r == 1))
                    last.then_inc(s1_done, 1)

            def coefficients(m):
                pe.wait_ge(kb_done, m + 1)
                if from_(m, 1):
                    pe.wait_ge(coef_used, m)
                nc.tensor.matmul(ps[:, B_COEF, 0:ND + NA], kb[:, :], k_narrow[:, 0:ND + NA], start=True, stop=True)
                nc.tensor.matmul(ps[:, B_COEF + 1, 0:NB], kb[:, :], k_narrow[:, ND + NA:O_MA],
                                 start=True, stop=True).then_inc(coef_done, 1)

            def stage2(n):
                pe.wait_ge(y_out, (n + 1) * NG1)
                if from_(n, 1):
                    pe.wait_ge(data_out, n)
                for sq in range(SQ):
                    for cs in range(2):
                        nc.tensor.matmul(ps[:, B_DATA, sq * NU:(sq + 1) * NU],
                                         y_sb[:, (sq * 2 + cs) * J:(sq * 2 + cs + 1) * J, :],
                                         const(O_RU + ((sq // Q) * 2 + cs) * NU, (1, NU)),
                                         start=(cs == 0), stop=(cs == 1))
                for r in range(2):
                    at = SQ * NU + r * NEDGE
                    last = nc.tensor.matmul(ps[:, B_DATA, at:at + NEDGE],
                                            y_sb[:, NP - 2 * J + r * J:NP - J + r * J, :],
                                            const(O_RE, (1, NEDGE)), start=True, stop=True)
                last.then_inc(s2_done, 1)

            def filter_logits(n):
                if not from_(n, 1):
                    pe.wait_ge(params_in, 32)
                pe.wait_ge(pool_done, n + 1)
                if from_(n, 1):
                    pe.wait_ge(k_step, (n - 1) * K_LINKS + 1)
                nc.tensor.matmul(ps[0:KROWS, B_LF, 0:GROUPS * TAPS], view(pooled[:, 0:1], (0, KROWS)),
                                 conv_sb[:, :], start=True, stop=True).then_inc(lf_done, 1)

            def load_step(n, it, u):
                stage1(n, it, u)
                if from_(n, 1):
                    coefficients(n - 1)
                stage2(n)
                filter_logits(n)

            pe.wait_ge(consts_in, 16)
            for u in range(2):
                load_step(u, 0, u)
            with pe.Fori(1, N // 2) as it:
                for u in range(2):
                    load_step(it * 2 + u, it, u)
            coefficients(N - 1)

            pe.wait_ge(weights_in, 16)
            pe.wait_ge(rest_in, 16)
            pe.wait_ge(eo_dve, 1)
            pe.wait_ge(eo_pool, 3)
            for b in range(MODES):
                for q in range(Q):
                    at = (b % 8) * 2 * J * N
                    for s in range(S):
                        last = nc.tensor.matmul(
                            view(ps[q * C:(q + 1) * C, b // 8, at:at + 1], (1, 2 * J * N)),
                            w_sb[:, s, q * MODES + b, :],
                            mixin[:, q * MODES + b, :, 1 - s:3 - s, :], start=(s == 0), stop=(s == 1))
                if b % 8 == 7 or b == MODES - 1:
                    last.then_inc(mix_done, 1)

            def to_modes(n, u):
                pe.wait_ge(pick_done, n + 1)
                if from_(n, 1):
                    pe.wait_ge(modes_act, n)
                    pe.wait_ge(modes_dve, n)
                for sj in range(S * J):
                    last = nc.tensor.matmul(
                        view(ps[:, B_TR + sj // J, (sj % J) * Q * C:(sj % J) * Q * C + 1], (1, Q * C)),
                        mixed_n[:, u, sj, :],
                        const(O_BC, (1, Q * C), rows_=Q * C), start=True, stop=True)
                last.then_inc(tr_done, 1)

            def to_columns(n, u):
                pe.wait_ge(modes_act, n + 1)
                pe.wait_ge(modes_dve, n + 1)
                if from_(n, 1):
                    pe.wait_ge(cols_act, n)
                    pe.wait_ge(cols_dve, n)
                for t in range(TRIPLES):
                    last = nc.tensor.matmul(ps[0:3 * NF, B_T + t // 6, (t % 6) * NW:(t % 6 + 1) * NW],
                                            modes[:, u, 3 * t:3 * t + 3, :], const(O_TW, (1, NW)),
                                            start=True, stop=True)
                    if t in (5, TRIPLES - 1):
                        last.then_inc(t_done, 1)

            def to_rows(n, u):
                pe.wait_ge(cols_act, n + 1)
                pe.wait_ge(cols_dve, n + 1)
                for k, (s, t, nt) in enumerate(CHUNKS):
                    if k >= 3:
                        pe.wait_ge(rows_dve if k % 2 == 0 else rows_act, n * 3 + (k - 3) // 2 + 1)
                    elif from_(n, 1):
                        pe.wait_ge(rows_dve if k % 2 == 0 else rows_act, (n - 1) * 3 + (k + 3) // 2 + 1)
                    nc.tensor.matmul(ps[:, B_F[k % 3], 0:nt * NW],
                                     const(O_LH + s * H, (1, H), rows_=3 * NF), cols[:, u, t:t + nt, :],
                                     start=True, stop=True).then_inc(f_done, 1)

            pe.wait_ge(mixed_act, 1)
            pe.wait_ge(mixed_dve, 1)
            to_modes(0, 0)
            to_modes(1, 1)
            to_columns(0, 0)
            for n in (1, 2):
                to_modes(n + 1, (n + 1) % 2)
                to_columns(n, n % 2)
                to_rows(n - 1, (n - 1) % 2)
            with pe.Fori(1, 3) as it:
                for u in (1, 0):
                    n = it * 2 + (2 - u)
                    to_modes(n + 1, 1 - u)
                    to_columns(n, u)
                    to_rows(n - 1, 1 - u)
            to_columns(N - 1, 1)
            to_rows(N - 2, 0)
            to_rows(N - 1, 1)

        def place_modes(copy, quadrants, u, sem_done):
            for quad in quadrants:
                cs, v = quad // 2, quad % 2
                part = slice(32 * quad, 32 * quad + 32)
                copy(view(modes[part, u, 0, 2 * v + cs:2 * v + cs + 1], (2, MODES // 2 + 1), (NF, C)),
                     view(ps[part, B_TR, 0:1], (C, MODES // 2 + 1), (1, C)))
                top = 2 * (MODES - 1 + v) + cs
                last = copy(view(modes[part, u, 0, top:top + 1], (-2, MODES // 2 - 1), (NF, C)),
                            view(ps[part, B_TR + 1, C:C + 1], (C, MODES // 2 - 1), (1, C)))
            last.then_inc(sem_done, 1)

        def place_rows(copy, k, u):
            s, t, nt = CHUNKS[k]
            return copy(view(rows[:, u, 3 * t + s, 0:1], (3 * H, nt), (H - HALF, 2), (1, HALF)),
                        view(ps[:, B_F[k % 3], 0:1], (NW, nt), (HALF, 2), (1, HALF)))

        def unmix(copy, bank):
            b0, nb = bank * 8, min(8, MODES - bank * 8)
            copy(view(mixed[:, 0, 0, b0:b0 + 1], (BPAD, J), (S * J * BPAD, N), (1, nb)),
                 view(ps[0:Q * C, bank, 0:1], (2 * N, J), (1, N), (2 * J * N, nb)))
            skip = 0
            if bank == 0:
                skip = 1
                copy(view(mixed[:, 0, J, 0:1], (BPAD, J), (S * J * BPAD, N)),
                     view(ps[0:Q * C, 0, N:N + 1], (2 * N, J), (1, N)))
            first, at = MODES - b0 - skip, N + skip * 2 * J * N
            return copy(view(mixed[:, 0, J, first:first + 1], (BPAD, J), (S * J * BPAD, N), (-1, nb - skip)),
                        view(ps[0:Q * C, bank, at:at + 1], (2 * N, J), (1, N), (2 * J * N, nb - skip)))

        def odd_even(tt, j, e):
            part = slice(C * j, C * j + C)
            half = Q * MODES
            a = view(acc[part, 0, 0:1], (1, half), (PLANE, N))
            b = view(acc[part, 0, half:half + 1], (1, half), (PLANE, N))
            o = view(mixin[part, 0, j, e, 0:1], (J * 3 * N, half), (1, N))
            if e == 1:
                return tt(o, a, b, ALU.add)
            return tt(o, *((a, b) if e == 0 else (b, a)), ALU.subtract)

        @block.scalar
        def _(act):
            act.wait_ge(setup, 1)
            nc.scalar.activation(bn[:, 0, :], bn[:, 1, :], ACT.Sqrt).then_inc(root_done, 1)

            def load_step(n, it, u):
                for g in range(NG1):
                    act.wait_ge(s1_done, n * NG1 + g + 1)
                    nc.scalar.copy(view(y_sb[:, 0, g * G1:g * G1 + 1], (1, G1), (C, NP)),
                                   view(ps[:, g, 0:1], (NP, G1), (1, NP))).then_inc(y_out, 1)
                act.wait_ge(s2_done, n + 1)
                nc.scalar.mul(pooled[:, :], ps[0:C, B_DATA, 0:1], 1.0 / (H * H)).then_inc(pool_done, 1)
                nc.scalar.copy(data[:, u, :], ps[:, B_DATA, 0:NDATA]).then_inc(data_out, 1)
                act.wait_ge(bn_done, n + 1)
                nc.scalar.activation(lf_tanh[:, :], lf_bn[:, :], ACT.Tanh).then_inc(tanh_done, 1)

            for u in range(2):
                load_step(u, 0, u)
            with act.Fori(1, N // 2) as it:
                for u in range(2):
                    load_step(it * 2 + u, it, u)

            act.wait_ge(zeroed, 1)
            act.wait_ge(mix_done, 1)
            unmix(nc.scalar.copy, 0)
            act.wait_ge(mix_done, 3)
            unmix(nc.scalar.copy, 2).then_inc(mixed_act, 1)

            def modes_step(n, u):
                act.wait_ge(tr_done, n + 1)
                place_modes(nc.scalar.copy, (0, 1), u, modes_act)

            def cols_step(n, u):
                act.wait_ge(t_done, n * 2 + 1)
                nc.scalar.copy(cols[:, u, 0:6, :], ps[0:3 * NF, B_T, 0:6 * NW]).then_inc(cols_act, 1)

            def rows_step(n, u):
                for k in (0, 2, 4):
                    act.wait_ge(f_done, n * 6 + k + 1)
                    if k == 0 and from_(n, 2):
                        act.wait_ge(out_done[u], ((n - u) // 2 if isinstance(n, int) else 0) * 16)
                    place_rows(nc.scalar.copy, k, u).then_inc(rows_act, 1)

            act.wait_ge(zeroed, 2)
            modes_step(0, 0)
            modes_step(1, 1)
            cols_step(0, 0)
            for n in (1, 2):
                modes_step(n + 1, (n + 1) % 2)
                cols_step(n, n % 2)
                rows_step(n - 1, (n - 1) % 2)
            with act.Fori(1, 3) as it:
                for u in (1, 0):
                    n = it * 2 + (2 - u)
                    modes_step(n + 1, 1 - u)
                    cols_step(n, u)
                    act.wait_ge(out_done[1 - u], it * 16)
                    rows_step(n - 1, 1 - u)
            cols_step(N - 1, 1)
            rows_step(N - 2, 0)
            rows_step(N - 1, 1)

        @block.vector
        def _(dve):
            tt, tr = nc.vector.tensor_tensor, nc.vector.tensor_reduce
            dve.wait_ge(params_in, 32)
            dve.wait_ge(narrow_in, 16)
            par_g = [par[:, o:o + GROUPS] for o in (P_GAMMA, P_BETA, P_MEAN, P_VAR)]
            nc.vector.tensor_scalar(bn[:, 1, :], par_g[3], 1e-5, None, ALU.add).then_inc(setup, 1)
            nc.vector.scalar_tensor_tensor(gain[:, 0, :], par[:, P_IN:P_IN + C], 1.0, par[:, P_L:P_L + C],
                                           op0=ALU.add, op1=ALU.mult)
            tt(gain[:, 1, :], par[:, P_IN:P_IN + C], par[:, P_L:P_L + C], ALU.mult)
            nc.vector.tensor_scalar(gain[:, 2, :], par[:, P_H:P_H + C], 1.0, None, ALU.add).then_inc(setup, 1)
            dve.wait_ge(root_done, 1)
            nc.vector.reciprocal(lf[:, :], bn[:, 0, :]).then_inc(setup, 1)
            dve.wait_ge(setup, 3)

            def gains(i):
                return view(gain[:, i, 0:1], (0, J), (1, C))

            tt(bn[:, 0, :], par_g[0], lf[:, :], ALU.mult).then_inc(setup, 1)
            tt(view(kb_mul[:, 0:1], (C, J), (1, C)), gains(0),
               view(k_narrow[:, O_MA:O_MA + 1], (C, J), (1, C)), ALU.mult)
            tt(view(kb_add[:, 0:1], (C, J), (1, C)), gains(1),
               view(k_narrow[:, O_MC:O_MC + 1], (C, J), (1, C)), ALU.mult)
            tt(view(kb_tmp[:, 0:1], (C, J), (1, C)), gains(2),
               view(k_narrow[:, O_MB:O_MB + 1], (C, J), (1, C)), ALU.mult).then_inc(setup, 1)
            dve.wait_ge(setup, 5)
            tt(kb_add[:, :], kb_add[:, :], kb_tmp[:, :], ALU.add)
            tt(pick[:, :, :], view(bn[:, 0, 0:1], (1, GROUPS), (0, TAPS)),
               view(k_narrow[:, O_PICK:O_PICK + 1], (TAPS, GROUPS), (1, TAPS)), ALU.mult)
            tt(lf_bn[:, :], par_g[2], bn[:, 0, :], ALU.mult).then_inc(setup, 1)
            dve.wait_ge(setup, 6)
            tt(bn[:, 1, :], par_g[1], lf_bn[:, :], ALU.subtract).then_inc(setup, 1)
            dve.wait_ge(setup, 7)

            def taps(n):
                base = n * K_LINKS

                dve.wait_ge(lf_done, n + 1)
                tt(lf_all[:, :], ps[0:KROWS, B_LF, 0:GROUPS * TAPS],
                   view(pick[:, 0, 0:1], (1, GROUPS * TAPS)), ALU.mult).then_inc(k_step, 1)
                dve.wait_ge(k_step, base + 1)
                tr(lf[:, :], view(lf_all[:, 0:1], (TAPS, GROUPS), (1, TAPS)), AX.X, ALU.add).then_inc(k_step, 1)
                dve.wait_ge(k_step, base + 2)
                tt(lf_bn[:, :], lf[:, :], bn[:, 1, :], ALU.add).then_inc(bn_done, 1)
                dve.wait_ge(tanh_done, n + 1)
                tt(view(kb_tmp[:, 0:1], (C, J), (J, GROUPS), (1, C // GROUPS)),
                   view(lf_tanh[:, 0:1], (0, J), (1, GROUPS), (0, C // GROUPS)),
                   view(kb_mul[:, 0:1], (C, J), (J, GROUPS), (1, C // GROUPS)), ALU.mult).then_inc(k_step, 1)
                dve.wait_ge(k_step, base + 3)
                tt(kb[:, :], kb_tmp[:, :], kb_add[:, :], ALU.add).then_inc(kb_done, 1)

            def combine(m, u):
                base = m * F_LINKS
                entry = lambda at, *dims: view(data[:, u, at:at + 1], *dims)
                low = lambda at, *dims: view(ps[:, B_COEF, at:at + 1], *dims)
                edge = SQ * NU

                dve.wait_ge(coef_done, m + 1)
                dve.wait_ge(data_out, m + 1)
                tt(view(prod_a[:, 0, 0:1], (8 * SQ, 3), (8, SQ), (1, 4)), entry(2 * MODES, (0, 3), (NU, SQ), (1, 4)),
                   low(ND, (8 * SQ, 3), (8, SQ), (1, 4)), ALU.mult)
                tt(view(prod_a[:, 0, 4:5], (8, 3 * SQ), (1, 4)),
                   entry(edge + NEDGE // 2 - 1, (0, 3 * SQ), (NEDGE // 2, 4)),
                   low(ND + 4, (8, 3 * SQ), (1, 4)), ALU.mult).then_inc(f_step, 1)
                tt(view(terms[:, 0, 0:1], (MODES, SQ), (PLANE, 2), (1, MODES)),
                   entry(0, (NU, SQ), (MODES, 2), (1, MODES)),
                   low(0, (MODES, SQ), (PLANE, 2), (1, MODES)), ALU.mult)
                for s in range(S):
                    at = s * Q * MODES
                    last = tt(view(terms[:, 2, at:at + 1], (PLANE, 4), (MODES, Q), (1, MODES)),
                              entry(edge + s * MODES, (NEDGE // 2, 4), (0, Q), (1, MODES)),
                              view(ps[:, B_COEF + 1, at:at + 1], (PLANE, 4), (MODES, Q), (1, MODES)), ALU.mult)
                last.then_inc(coef_used, 1)
                dve.wait_ge(f_step, base + 1)
                tr(coef_a[:, :], prod_a[:, :, :], AX.X, ALU.add).then_inc(f_step, 1)
                dve.wait_ge(f_step, base + 2)
                tt(view(terms[:, 6, 0:1], (MODES, 3 * SQ), (1, MODES)), view(coef_a[:, 0:1], (1, 3 * SQ), (0, MODES)),
                   const(O_BAS, (MODES, 3 * SQ), (1, MODES)), ALU.mult).then_inc(f_step, 1)
                dve.wait_ge(f_step, base + 3)
                if from_(m, 2):
                    dve.wait_ge(acc_done, m - 1)
                tr(xht[:, u, :], view(terms[:, 0, 0:1], (1, PLANE), (PLANE, NTERM)), AX.X, ALU.add).then_inc(xht_done, 1)

            def load_step(n, it, u):
                if from_(n, 1):
                    combine(n - 1, 1 - u)
                taps(n)

            dve.wait_ge(rest_in, 16)
            for u in range(2):
                load_step(u, 0, u)
            with dve.Fori(1, N // 2) as it:
                for u in range(2):
                    load_step(it * 2 + u, it, u)
            combine(N - 1, 1)

            dve.wait_ge(acc_done, N)
            dve.wait_ge(zeroed, 1)
            for j in (0, 1, 2):
                for e in range(3):
                    last = odd_even(tt, j, e)
            last.then_inc(eo_dve, 1)

            dve.wait_ge(mix_done, 2)
            unmix(nc.vector.tensor_copy, 1).then_inc(mixed_dve, 1)

            def modes_step(n, u):
                dve.wait_ge(tr_done, n + 1)
                place_modes(nc.vector.tensor_copy, (2, 3), u, modes_dve)

            def cols_step(n, u):
                dve.wait_ge(t_done, n * 2 + 2)
                nc.vector.tensor_copy(cols[:, u, 6:TRIPLES, :],
                                      ps[0:3 * NF, B_T + 1, 0:(TRIPLES - 6) * NW]).then_inc(cols_dve, 1)

            def rows_step(n, u):
                for k in (1, 3, 5):
                    dve.wait_ge(f_done, n * 6 + k + 1)
                    place_rows(nc.vector.tensor_copy, k, u).then_inc(rows_dve, 1)

            dve.wait_ge(zeroed, 2)
            modes_step(0, 0)
            modes_step(1, 1)
            cols_step(0, 0)
            for n in (1, 2):
                modes_step(n + 1, (n + 1) % 2)
                cols_step(n, n % 2)
                rows_step(n - 1, (n - 1) % 2)
            with dve.Fori(1, 3) as it:
                for u in (1, 0):
                    n = it * 2 + (2 - u)
                    modes_step(n + 1, 1 - u)
                    cols_step(n, u)
                    dve.wait_ge(out_done[1 - u], it * 16)
                    rows_step(n - 1, 1 - u)
            cols_step(N - 1, 1)
            for n in (N - 2, N - 1):
                dve.wait_ge(out_done[n % 2], (n // 2) * 16)
                rows_step(n, n % 2)

        @block.gpsimd
        def _(pool):
            tt = nc.gpsimd.tensor_tensor
            nc.gpsimd.memset(mixin[:, :, :, :, :], 0.0)
            nc.gpsimd.memset(mixed[:, :, :, :], 0.0).then_inc(zeroed, 1)
            nc.gpsimd.memset(modes[:, :, :, :], 0.0)
            nc.gpsimd.memset(rows[:, :, :, :], 0.0).then_inc(zeroed, 1)
            pool.wait_ge(rest_in, 16)

            def spread_step(n, u):
                pool.wait_ge(xht_done, n + 1)
                src = view(xht[:, u, 0:1], (0, N), (1, PLANE))
                if isinstance(n, int):
                    at = k_wide[:, O_BT + n * N:O_BT + n * N + 1]
                else:
                    at = k_wide[:, bass.ds(n * N + O_BT, 1)]
                weight = view(at, (1, N), (0, PLANE))
                if not from_(n, 1):
                    tt(acc[:, :, :], src, weight, ALU.mult).then_inc(acc_done, 1)
                    return
                pool.wait_ge(acc_done, n)
                tt(spread[:, :, :], src, weight, ALU.mult).then_inc(spread_done, 1)
                pool.wait_ge(spread_done, n)
                tt(acc[:, :, :], acc[:, :, :], spread[:, :, :], ALU.add).then_inc(acc_done, 1)

            for u in range(2):
                spread_step(u, u)
            with pool.Fori(1, N // 2) as it:
                for u in range(2):
                    spread_step(it * 2 + u, u)
            pool.wait_ge(acc_done, N)
            pool.wait_ge(zeroed, 2)
            for e in range(3):
                odd_even(tt, 3, e).then_inc(eo_pool, 1)
            pool.wait_ge(eo_pool, 3)

            def pick_step(n, u):
                if from_(n, 2):
                    pool.wait_ge(tr_done, n - 1)
                src = mixed[:, n, :, :] if isinstance(n, int) else mixed[:, bass.ds(n, 1), :, :]
                nc.gpsimd.tensor_copy(view(mixed_n[:, u, 0, 0:1], (4 * BPAD, S * J), (BPAD, 4), (1, BPAD)),
                                      view(src, (BPAD, S * J), (0, 4), (1, BPAD))).then_inc(pick_done, 1)

            pool.wait_ge(mixed_act, 1)
            pool.wait_ge(mixed_dve, 1)
            for u in range(2):
                pick_step(u, u)
            with pool.Fori(1, N // 2) as it:
                for u in range(2):
                    pick_step(it * 2 + u, u)


def kernel(**inputs):
    import concourse.bacc as bacc
    from concourse.bass_utils import run_bass_kernel_spmd

    wide, narrow = constants()
    w1 = np.asarray(inputs["L1_conv_w1"])
    a_at = np.array([[[frequency(s, j, q) for q in range(Q)] for s in range(S)] for j in range(J)])
    b_at = np.array([[column(s, b) for b in range(MODES)] for s in range(S)])
    mix_w = w1[:, :, a_at[:, :, :, None], b_at[None, :, None, :]]
    mix_w = np.ascontiguousarray(mix_w.transpose(2, 0, 3, 4, 5, 1)).reshape(J * C, S, Q * MODES, C)

    def per_channel(a):
        return np.broadcast_to(np.asarray(a).reshape(1, C), (KROWS, C))

    def per_tap(a):
        a = np.asarray(a).reshape(GROUPS, TAPS).T
        return np.repeat(np.concatenate([a, a[:1]], 0), J, axis=0)

    params = np.concatenate(
        [per_channel(inputs[f"L0_conv_{k}"]) for k in ("lamb_l", "lamb_h", "inside_all")]
        + [per_tap(inputs[f"L0_conv_bn_{k}"]) for k in ("gamma", "beta", "mean", "var")], 1)
    arrays = {
        "x": np.ascontiguousarray(inputs["x"]),
        "wide": wide,
        "narrow": narrow,
        "params": np.ascontiguousarray(params),
        "conv_wt": np.ascontiguousarray(np.asarray(inputs["L0_conv_conv_w"]).T),
        "mix_w": mix_w,
    }
    nc = bacc.Bacc("TRN2", target_bir_lowering=False, num_devices=1)
    args = [nc.dram_tensor(k, a.shape, mybir.dt.from_np(a.dtype), kind="ExternalInput").ap()
            for k, a in arrays.items()]
    out = nc.dram_tensor("out", (N, C, H, H), mybir.dt.float32, kind="ExternalOutput").ap()
    hartley_conv_kernel(nc, *args, out)
    result = run_bass_kernel_spmd(nc, [arrays], core_ids=[0])
    return result.results[0]["out"]
```

```python
from contextlib import ExitStack

import numpy as np

import concourse.bass as bass
from concourse import mybir

N, C, H = 8, 32, 128
MODES = 20
GROUPS, TAPS = 8, 9
J, Q, S = 4, 3, 2
SQ = S * Q
NP = SQ * 2 * J + 2 * J
NU = 2 * MODES + 4
NEDGE = 2 * (S * MODES + 1)
NDATA = SQ * NU + 2 * NEDGE
KT = TAPS + 1
KROWS = KT * J
PLANE = SQ * MODES
ND, NA, NB = 2 * PLANE, 3 * SQ * 8, 4 * PLANE
NTERM = 9
HALF = 33
NW = 2 * HALF
NF = 21 * 2
TRIPLES = 11
BPAD = 32
REACH = 4
CPAD = C + 2 * REACH
WSHARES = N - 2
WSTEP = S * Q * MODES // WSHARES

O_LT, O_RU = 0, 4 * NP
O_RE = O_RU + S * 2 * NU
O_BAS = O_RE + NEDGE
O_BT = O_BAS + 3 * PLANE
O_TW = O_BT + N * N
O_LH = O_TW + NW
NC128 = O_LH + 3 * H
O_TAB = 0
O_MA = ND + NA + NB
O_MB, O_MC = O_MA + H, O_MA + 2 * H
O_PICK = O_MA + 3 * H
NC40 = O_PICK + GROUPS * TAPS
P_L, P_H, P_IN = 0, C, 2 * C
P_GAMMA = 3 * C
P_BETA, P_MEAN, P_VAR = P_GAMMA + GROUPS, P_GAMMA + 2 * GROUPS, P_GAMMA + 3 * GROUPS
NPAR = P_GAMMA + 4 * GROUPS


def frequency(s, j, q):
    a = min(Q * j + q, MODES // 2)
    return a if s == 0 else (MODES - a) % MODES


def column(s, b):
    return b if s == 0 else (MODES - b) % MODES


def gaussian():
    k = np.exp(-0.5 * np.arange(-REACH, REACH + 1, dtype=np.float32) ** 2)
    return (k / k.sum()).astype(np.float64)


def blur_matrix(n):
    k = gaussian()
    m = np.zeros((n, n))
    for o in range(n):
        for i in range(2 * REACH + 1):
            m[o, min(max(o + i - REACH, 0), n - 1)] += k[i]
    return m


def constants():
    th = 2 * np.pi / H
    h = np.arange(H)
    e1, e2 = np.zeros(H), np.zeros(H)
    e1[1], e1[H - 1] = 1, -1
    e2[H - 2], e2[0] = 1, -1
    lt = np.zeros((H, NP))
    ru = np.zeros((H, S, 2, NU))
    re = np.zeros((H, NEDGE))
    basis = np.zeros((3, S, Q, MODES))
    for s in range(S):
        for q in range(Q):
            for j in range(J):
                a = frequency(s, j, q)
                lt[:, ((s * Q + q) * 2) * J + j] = np.cos(th * a * h)
                lt[:, ((s * Q + q) * 2 + 1) * J + j] = np.sin(th * a * h)
        for b in range(MODES):
            bb = column(s, b)
            c, sn = np.cos(th * bb * h), np.sin(th * bb * h)
            ru[:, s, 0, b], ru[:, s, 0, MODES + b] = c, sn
            ru[:, s, 1, b], ru[:, s, 1, MODES + b] = -sn, c
            re[:, s * MODES + b], re[:, NEDGE // 2 + s * MODES + b] = c, sn
            basis[:, s, :, b] = np.array([1, np.cos(th * bb), np.sin(th * bb)])[:, None]
        ru[:, s, 0, 2 * MODES], ru[:, s, 0, 2 * MODES + 1] = e1, e2
        ru[:, s, 1, 2 * MODES + 2], ru[:, s, 1, 2 * MODES + 3] = e1, e2
    lt[:, NP - 2 * J:NP - J], lt[:, NP - J:] = e1[:, None], e2[:, None]
    re[:, NEDGE // 2 - 1], re[:, NEDGE - 1] = e1, e2

    d = np.zeros((KT, J, 2, S, Q, MODES))
    e = np.zeros((KT, J, 4, S, Q, MODES))
    f = np.zeros((KT, J, 3, S, Q, 8))
    for j in range(J):
        for s in range(S):
            for q in range(Q):
                a = frequency(s, j, q)
                ea = np.exp(1j * th * a)
                for b in range(MODES):
                    bb = column(s, b)
                    eb = np.exp(1j * th * bb)
                    g = 1 - 1j * np.conj(ea) * np.conj(eb)
                    for di in (-1, 0, 1):
                        for dj in (-1, 0, 1):
                            t = (di + 1) * 3 + dj + 1
                            k = g * ea ** di * eb ** dj
                            d[t, j, 0, s, q, b], d[t, j, 1, s, q, b] = k.real, k.imag
                            if di:
                                r = 0 if di < 0 else 2
                                z = g * (1 if di < 0 else ea) * eb ** dj
                                e[t, j, r, s, q, b], e[t, j, r + 1, s, q, b] = z.real, z.imag
                    if a == 0 and bb == 0:
                        d[TAPS, j, 0, s, q, b] = 1
                for di in (-1, 0, 1):
                    for dj in (-1, 1):
                        t, r = (di + 1) * 3 + dj + 1, (0 if dj < 0 else 1)
                        parts = [(r, ea ** di), (2 + r, -1j * ea ** di)]
                        if di:
                            parts.append((4 + (0 if di < 0 else 2) + r, 1 if di < 0 else ea))
                        for k, z in parts:
                            m = ([z, -1j * z * np.conj(ea), -z * np.conj(ea)] if dj < 0
                                 else [-1j * np.conj(ea) * z, z, 1j * z])
                            f[t, j, :, s, q, k] = np.real(m)
    table = np.concatenate([d.reshape(KROWS, ND), f.reshape(KROWS, NA), e.reshape(KROWS, NB)], 1)

    kept = np.concatenate([np.arange(HALF), np.arange(H - HALF, H)])
    tw = np.zeros((2, 2, BPAD, H))
    for b in range(MODES):
        tw[0, 0, b], tw[0, 1, b] = np.cos(th * h * b), -np.sin(th * h * (b + 1))
        tw[1, 0, b], tw[1, 1, b] = -np.sin(th * h * b), -np.cos(th * h * (b + 1))
    rows = blur_matrix(H)
    tw = (tw.reshape(128, H) @ rows.T)[:, kept] * (0.5 / (H * H) * gaussian()[-1])
    tw[:, HALF] = 0
    lh = np.zeros((3, 128, H))
    for s in range(3):
        for a in range(MODES + 1):
            lh[s, s * NF + 2 * a] = rows @ np.cos(th * h * a)
            lh[s, s * NF + 2 * a + 1] = rows @ np.sin(th * h * a)

    wide = np.zeros((128, NC128), np.float32)
    pair = np.zeros((2, H // 2, 2, 2, NP))
    for i in range(2):
        pair[i, :, :, i] = lt.reshape(H // 2, 2, NP)
    wide[:, O_LT:O_RU] = pair.reshape(H, 4 * NP)
    wide[:, O_RU:O_RE] = ru.reshape(H, -1)
    wide[:, O_RE:O_BAS] = re
    wide[:, O_BAS:O_BT] = basis.reshape(1, -1)
    wide[:, O_BT:O_TW] = blur_matrix(N).T.reshape(1, -1)
    wide[:, O_TW:O_LH] = tw
    wide[:, O_LH:] = lh.transpose(1, 0, 2).reshape(128, -1)

    t, own = np.arange(KROWS) // J, np.kron(np.arange(KROWS) % J, 1)[:, None] == (np.arange(128) // C)[None]
    narrow = np.zeros((KROWS, NC40), np.float32)
    narrow[:, O_TAB:O_MA] = table
    narrow[:, O_MA:O_MB] = own * (t < TAPS)[:, None]
    narrow[:, O_MB:O_MC] = own * (t == TAPS // 2)[:, None]
    narrow[:, O_MC:O_PICK] = -1.0 * own * (t == TAPS)[:, None]
    narrow[:, O_PICK:] = np.tile(t[:, None] == np.arange(TAPS)[None], (1, GROUPS))
    return wide, narrow


def hartley_conv_kernel(nc, x, wide, narrow, params, conv_wt, mix_w, out):
    fp32 = mybir.dt.float32
    ALU = mybir.AluOpType
    ACT = mybir.ActivationFunctionType
    AX = mybir.AxisListType
    HC = C // 2
    G1 = 8
    NG1 = C // G1

    def view(ap, *dims):
        return bass.AP(tensor=ap.tensor, offset=ap.offset, ap=[ap.ap[0], *[list(d) for d in dims]])

    def from_(n, least):
        return not isinstance(n, int) or n >= least

    ctx = ExitStack()
    with ctx:
        def sb(name, shape):
            return ctx.enter_context(nc.sbuf_tensor(name, shape, fp32))

        def sem(name):
            return ctx.enter_context(nc.semaphore(name))

        x_ring = sb("x_ring", [H, 2, C // 2, 2 * H])
        mixed_t = x_ring[:, 0]
        k_wide = sb("k_wide", [128, NC128])
        k_narrow = sb("k_narrow", [KROWS, NC40])
        par = sb("par", [KROWS, NPAR])
        conv_sb = sb("conv_sb", [C, GROUPS * TAPS])
        w_raw = sb("w_raw", [128, S * Q * MODES, CPAD])
        w_acc = sb("w_acc", [128, WSTEP * C])
        w_pair = sb("w_pair", [128, REACH, WSTEP, C])
        w_sb = sb("w_sb", [128, S * Q * MODES, C])
        y_sb = sb("y_sb", [H, 2, NP, C])
        data = sb("data", [128, 2, NDATA])
        pooled = sb("pooled", [C, 1])
        bn = sb("bn", [KROWS, 2, GROUPS])
        gain = sb("gain", [KROWS, 3, C])
        pick = sb("pick", [KROWS, GROUPS, TAPS])
        kb_mul = sb("kb_mul", [KROWS, 128])
        kb_add = sb("kb_add", [KROWS, 128])
        kb_tmp = sb("kb_tmp", [KROWS, 128])
        kb = sb("kb", [KROWS, 128])
        lf_all = sb("lf_all", [KROWS, GROUPS * TAPS])
        lf = sb("lf", [KROWS, GROUPS])
        lf_bn = sb("lf_bn", [KROWS, GROUPS])
        lf_tanh = sb("lf_tanh", [KROWS, GROUPS])
        prod_a = sb("prod_a", [128, 3 * SQ, 8])
        coef_a = sb("coef_a", [128, 3 * SQ])
        terms = sb("terms", [128, NTERM, PLANE])
        xht = sb("xht", [128, PLANE])
        parts = sb("parts", [128, 2, 2, Q * MODES])
        spread = sb("spread", [128, N, PLANE])
        acc = sb("acc", [128, N, PLANE])
        idle = sb("idle", [128, 512])
        mixin = sb("mixin", [128, Q * MODES, J, 3, N])
        mixed = sb("mixed", [Q * C, N, S * J, BPAD])
        modes = sb("modes", [128, 2, C + 1, NF])
        cols = sb("cols", [3 * NF, 2, TRIPLES, NW])
        rows = sb("rows", [H, 2, C, H])
        ps = ctx.enter_context(nc.psum_tensor("ps", [128, 8, 512], fp32))

        consts_in, params_in, narrow_in, rest_in, weights_in = map(
            sem, ("consts_in", "params_in", "narrow_in", "rest_in", "weights_in"))
        x_in = [sem(f"x_in{i}") for i in range(4)]
        x_first, idle_ready = sem("x_first"), sem("idle_ready")
        s1_done, y_out, s2_first, s2_done, pool_done, data_out = map(
            sem, ("s1_done", "y_out", "s2_first", "s2_done", "pool_done", "data_out"))
        setup, root_done, lf_done, k_step, bn_done, tanh_done, kb_done = map(
            sem, ("setup", "root_done", "lf_done", "k_step", "bn_done", "tanh_done", "kb_done"))
        coef_done, coef_used, f_step, parts_done, spread_done, acc_done, last_share = map(
            sem, ("coef_done", "coef_used", "f_step", "parts_done", "spread_done", "acc_done", "last_share"))
        pairs_done, blur_step = map(sem, ("pairs_done", "blur_step"))
        zeroed, mixin_dve, mixin_act, mix_done, mixed_act, mixed_dve = map(
            sem, ("zeroed", "mixin_dve", "mixin_act", "mix_done", "mixed_act", "mixed_dve"))
        turned, modes_act, modes_dve, t_done, cols_act, cols_dve = map(
            sem, ("turned", "modes_act", "modes_dve", "t_done", "cols_act", "cols_dve"))
        f_done, rows_act, rows_dve = map(sem, ("f_done", "rows_act", "rows_dve"))
        out_done = [sem(f"out_done{i}") for i in range(2)]

        B_DATA, B_LF, B_COEF = 4, 5, 6
        B_T, B_F = 3, (5, 6, 7)
        K_LINKS, F_LINKS = 3, 5

        wide_row = k_wide[:, 0:1]

        def const(offset, *dims, rows_=128):
            return view(k_wide[0:rows_, offset:offset + 1], *dims)

        block = ctx.enter_context(nc.Block())

        CHUNKS = [(s, t, (6 if t == 0 else (5 if s < 2 else 4))) for t in (0, 6) for s in range(3)]
        FIRST = 18
        PLACED = (1, 3, 3, 4, 5, 5)
        ROUND = 5

        def data_at(sq):
            if sq == 0:
                return ps[:, B_LF, GROUPS * TAPS:GROUPS * TAPS + NU]
            return ps[:, B_DATA, sq * NU:(sq + 1) * NU]

        @block.sync
        def _(sp):
            pairs = x.rearrange("n (k s) (p r) w -> n (s p) k (r w)", s=2, r=2)

            def load(n, u, half):
                if from_(n, 2):
                    sp.wait_ge(s1_done, (n - 2) * NG1 + (half + 1) * NG1 // 2)
                sp.dma_start(x_ring[:, u, half * HC // 2:(half + 1) * HC // 2, :],
                             pairs[n, :, half * HC // 2:(half + 1) * HC // 2, :]).then_inc(x_in[2 * u + half], 16)

            sp.dma_start(k_wide[:, 0:O_BAS], wide[:, 0:O_BAS]).then_inc(consts_in, 16)
            sp.dma_start(x_ring[:, 0, 0:HC // 4, :], pairs[0, :, 0:HC // 4, :]).then_inc(x_first, 16)
            sp.dma_start(x_ring[:, 0, HC // 4:HC // 2, :], pairs[0, :, HC // 4:HC // 2, :]).then_inc(x_in[0], 16)
            load(0, 0, 1)
            load(1, 1, 0)
            sp.dma_start(par[:, :], params).then_inc(params_in, 16)
            sp.dma_start(conv_sb[:, :], conv_wt).then_inc(params_in, 16)
            sp.dma_start(k_narrow[:, :], narrow).then_inc(narrow_in, 16)
            load(1, 1, 1)
            sp.dma_start(k_wide[:, O_BAS:], wide[:, O_BAS:]).then_inc(rest_in, 16)
            load(2, 0, 0)
            sp.dma_start(w_raw[:, :, :], mix_w).then_inc(weights_in, 16)
            load(2, 0, 1)
            for n in range(3, N):
                for half in range(2):
                    load(n, n % 2, half)

            def store(n, u):
                for lo, hi, placed in ((0, FIRST, PLACED[1]), (FIRST, C, ROUND)):
                    sp.wait_ge(rows_act, n * ROUND + placed)
                    sp.wait_ge(rows_dve, n * ROUND + placed)
                    dst = out[bass.ds(n, 1), lo:hi, :, :]
                    sp.dma_start(dst.rearrange("a c h w -> h (a c) w"), rows[:, u, lo:hi, :]
                                 ).then_inc(out_done[u], 16)

            with sp.Fori(0, N // 2) as it:
                for u in range(2):
                    store(it * 2 + u, u)
            for u in range(2):
                sp.wait_ge(out_done[u], 32 * (N // 2))

        @block.tensor
        def _(pe):
            def keep_busy(count):
                for _ in range(count):
                    nc.tensor.matmul(ps[:, 0, :], idle[:, 0:128], idle[:, :], start=True, stop=True)

            def stage1(n, it, u, g):
                if isinstance(n, int) and n == 0 and g == 0:
                    pe.wait_ge(x_first, 16)
                elif g % 2 == 0 or (isinstance(n, int) and n == 0):
                    pe.wait_ge(x_in[2 * u + g // 2], it * 16 + 16)
                if from_(n, 1):
                    pe.wait_ge(y_out, (n - 1) * NG1 + g + 1)
                for i in range(G1 // 2):
                    for r in range(2):
                        last = nc.tensor.matmul(ps[:, g, 2 * i * NP:2 * (i + 1) * NP],
                                                x_ring[:, u, g * G1 // 2 + i, r * H:(r + 1) * H],
                                                const(O_LT + r * 2 * NP, (1, 2 * NP)),
                                                start=(r == 0), stop=(r == 1))
                last.then_inc(s1_done, 1)

            def coefficients(m):
                pe.wait_ge(kb_done, m + 1)
                if from_(m, 1):
                    pe.wait_ge(coef_used, m)
                nc.tensor.matmul(ps[:, B_COEF, 0:ND + NA], kb[:, :], k_narrow[:, 0:ND + NA], start=True, stop=True)
                nc.tensor.matmul(ps[:, B_COEF + 1, 0:NB], kb[:, :], k_narrow[:, ND + NA:O_MA],
                                 start=True, stop=True).then_inc(coef_done, 1)

            def stage2(n, u, quarter):
                if quarter == 0:
                    pe.wait_ge(y_out, (n + 1) * NG1)
                    if from_(n, 1):
                        pe.wait_ge(data_out, n)
                if quarter < 3:
                    for sq in (2 * quarter, 2 * quarter + 1):
                        for cs in range(2):
                            last = nc.tensor.matmul(data_at(sq),
                                                    y_sb[:, u, (sq * 2 + cs) * J:(sq * 2 + cs + 1) * J, :],
                                                    const(O_RU + ((sq // Q) * 2 + cs) * NU, (1, NU)),
                                                    start=(cs == 0), stop=(cs == 1))
                        if sq == 0:
                            last.then_inc(s2_first, 1)
                else:
                    for r in range(2):
                        at = SQ * NU + r * NEDGE
                        last = nc.tensor.matmul(ps[:, B_DATA, at:at + NEDGE],
                                                y_sb[:, u, NP - 2 * J + r * J:NP - J + r * J, :],
                                                const(O_RE, (1, NEDGE)), start=True, stop=True)
                    last.then_inc(s2_done, 1)

            def filter_logits(n):
                if not from_(n, 1):
                    pe.wait_ge(params_in, 32)
                pe.wait_ge(pool_done, n + 1)
                if from_(n, 1):
                    pe.wait_ge(k_step, (n - 1) * K_LINKS + 1)
                nc.tensor.matmul(ps[0:KROWS, B_LF, 0:GROUPS * TAPS], view(pooled[:, 0:1], (0, KROWS)),
                                 conv_sb[:, :], start=True, stop=True).then_inc(lf_done, 1)

            def load_step(n, it, u):
                stage1(n, it, u, 0)
                stage2(n - 1, 1 - u, 0)
                stage1(n, it, u, 1)
                filter_logits(n - 1)
                stage2(n - 1, 1 - u, 1)
                stage1(n, it, u, 2)
                coefficients(n - 1)
                stage2(n - 1, 1 - u, 2)
                stage1(n, it, u, 3)
                stage2(n - 1, 1 - u, 3)

            pe.wait_ge(idle_ready, 1)
            keep_busy(2)
            pe.wait_ge(consts_in, 16)
            for g in range(NG1):
                stage1(0, 0, 0, g)
            load_step(1, 0, 1)
            with pe.Fori(1, N // 2) as it:
                for u in range(2):
                    load_step(it * 2 + u, it, u)
            stage2(N - 1, 1, 0)
            filter_logits(N - 1)
            for quarter in (1, 2, 3):
                stage2(N - 1, 1, quarter)
            coefficients(N - 1)
            keep_busy(4)

            pe.wait_ge(rest_in, 16)
            pe.wait_ge(parts_done, N)
            keep_busy(4)
            pe.wait_ge(blur_step, WSHARES * REACH)
            pe.wait_ge(mixin_dve, 1)
            pe.wait_ge(mixin_act, 1)
            for b in range(MODES):
                for q in range(Q):
                    at = (b % 8) * 2 * J * N
                    for s in range(S):
                        last = nc.tensor.matmul(
                            view(ps[q * C:(q + 1) * C, b // 8, at:at + 1], (1, 2 * J * N)),
                            w_sb[:, (s * Q + q) * MODES + b, :],
                            mixin[:, q * MODES + b, :, 1 - s:3 - s, :], start=(s == 0), stop=(s == 1))
                if b % 8 == 7 or b == MODES - 1:
                    last.then_inc(mix_done, 1)

            def to_columns(n, u):
                pe.wait_ge(modes_act, n + 1)
                pe.wait_ge(modes_dve, n + 1)
                if from_(n, 1):
                    pe.wait_ge(cols_act, n)
                    pe.wait_ge(cols_dve, n)
                for t in range(TRIPLES):
                    last = nc.tensor.matmul(ps[0:3 * NF, B_T + t // 6, (t % 6) * NW:(t % 6 + 1) * NW],
                                            modes[:, u, 3 * t:3 * t + 3, :], const(O_TW, (1, NW)),
                                            start=True, stop=True)
                    if t in (5, TRIPLES - 1):
                        last.then_inc(t_done, 1)

            def to_rows(n, u):
                pe.wait_ge(cols_act, n + 1)
                pe.wait_ge(cols_dve, n + 1)
                for k, (s, t, nt) in enumerate(CHUNKS):
                    if k >= 3:
                        pe.wait_ge(rows_dve if k % 2 == 0 else rows_act, n * ROUND + PLACED[k - 3])
                    elif from_(n, 1):
                        pe.wait_ge(rows_dve if k % 2 == 0 else rows_act, (n - 1) * ROUND + PLACED[k + 3])
                    nc.tensor.matmul(ps[:, B_F[k % 3], 0:nt * NW],
                                     const(O_LH + s * H, (1, H), rows_=3 * NF), cols[:, u, t:t + nt, :],
                                     start=True, stop=True).then_inc(f_done, 1)

            pe.wait_ge(mixed_dve, 1)
            pe.wait_ge(mixed_act, 1)
            keep_busy(3)
            to_columns(0, 0)
            for n in (1, 2):
                to_columns(n, n % 2)
                to_rows(n - 1, (n - 1) % 2)
            with pe.Fori(1, 3) as it:
                for u in (1, 0):
                    n = it * 2 + (2 - u)
                    to_columns(n, u)
                    to_rows(n - 1, 1 - u)
            to_columns(N - 1, 1)
            to_rows(N - 2, 0)
            to_rows(N - 1, 1)

        def slot_view(n, part, sj, count):
            at = mixed_t[part, bass.ds(n, 1), sj * C:sj * C + 1]
            return view(at, (C, count), (1, C))

        def place_modes(copy, quadrants, n, u, sem_done):
            for quad in quadrants:
                cs, v = quad // 2, quad % 2
                part = slice(32 * quad, 32 * quad + 32)
                for q in range(Q):
                    rows_q = slice(q * C, q * C + C)
                    for s in range(S):
                        js = [j for j in range(J) if (Q * j + q <= MODES // 2 if s == 0
                                                      else 0 < Q * j + q < MODES // 2)]
                        c = Q * js[0] + q
                        at = 2 * ((c if s == 0 else MODES - c) + v) + cs
                        step = 2 * Q if s == 0 else -2 * Q
                        last = copy(view(modes[part, u, 0, at:at + 1], (step, len(js)), (NF, C)),
                                    slot_view(n, rows_q, s * J + js[0], len(js)))
            last.then_inc(sem_done, 1)

        def place_rows(copy, k, u):
            s, t, nt = CHUNKS[k]
            return copy(view(rows[:, u, 3 * t + s, 0:1], (3 * H, nt), (H - HALF, 2), (1, HALF)),
                        view(ps[:, B_F[k % 3], 0:1], (NW, nt), (HALF, 2), (1, HALF)))

        def unmix(copy, bank):
            b0, nb = bank * 8, min(8, MODES - bank * 8)
            copy(view(mixed[:, 0, 0, b0:b0 + 1], (BPAD, J), (S * J * BPAD, N), (1, nb)),
                 view(ps[0:Q * C, bank, 0:1], (2 * N, J), (1, N), (2 * J * N, nb)))
            skip = 0
            if bank == 0:
                skip = 1
                copy(view(mixed[:, 0, J, 0:1], (BPAD, J), (S * J * BPAD, N)),
                     view(ps[0:Q * C, 0, N:N + 1], (2 * N, J), (1, N)))
            first, at = MODES - b0 - skip, N + skip * 2 * J * N
            return copy(view(mixed[:, 0, J, first:first + 1], (BPAD, J), (S * J * BPAD, N), (-1, nb - skip)),
                        view(ps[0:Q * C, bank, at:at + 1], (2 * N, J), (1, N), (2 * J * N, nb - skip)))

        def place_parts(copy, j):
            part = slice(C * j, C * j + C)
            return copy(view(mixin[part, 0, j, 0, 0:1], (N, 2), (J * 3 * N, Q * MODES), (1, N)),
                        view(acc[part, 0, 0:1], (Q * MODES, 2), (1, Q * MODES), (PLANE, N)))

        def place_minus_odd(j):
            part = slice(C * j, C * j + C)
            return nc.scalar.mul(view(mixin[part, 0, j, 2, 0:1], (J * 3 * N, Q * MODES), (1, N)),
                                 view(acc[part, 0, 0:1], (1, Q * MODES), (PLANE, N)), -1.0)

        @block.scalar
        def _(act):
            act.wait_ge(setup, 1)
            nc.scalar.activation(bn[:, 0, :], bn[:, 1, :], ACT.Sqrt).then_inc(root_done, 1)

            def empty(n, u, g):
                act.wait_ge(s1_done, n * NG1 + g + 1)
                nc.scalar.copy(view(y_sb[:, u, 0, g * G1:g * G1 + 1], (1, G1), (C, NP)),
                               view(ps[:, g, 0:1], (NP, G1), (1, NP))).then_inc(y_out, 1)

            def pool(m, u):
                act.wait_ge(s2_first, m + 1)
                nc.scalar.copy(data[:, u, 0:NU], data_at(0))
                nc.scalar.mul(pooled[:, :], ps[0:C, B_LF, GROUPS * TAPS:GROUPS * TAPS + 1], 1.0 / (H * H)
                              ).then_inc(pool_done, 1)

            def tanh(m):
                act.wait_ge(bn_done, m + 1)
                nc.scalar.activation(lf_tanh[:, :], lf_bn[:, :], ACT.Tanh).then_inc(tanh_done, 1)

            def keep_data(m, u):
                act.wait_ge(s2_done, m + 1)
                nc.scalar.copy(data[:, u, NU:], ps[:, B_DATA, NU:NDATA]).then_inc(data_out, 1)

            def load_step(n, u):
                empty(n, u, 0)
                pool(n - 1, 1 - u)
                empty(n, u, 1)
                tanh(n - 1)
                empty(n, u, 2)
                empty(n, u, 3)
                keep_data(n - 1, 1 - u)

            for g in range(NG1):
                empty(0, 0, g)
            load_step(1, 1)
            with act.Fori(1, N // 2) as it:
                for u in range(2):
                    load_step(it * 2 + u, u)
            pool(N - 1, 1)
            tanh(N - 1)
            keep_data(N - 1, 1)

            act.wait_ge(last_share, 1)
            act.wait_ge(zeroed, 2)
            for j in range(J):
                place_minus_odd(j)
            place_parts(nc.scalar.copy, J - 1).then_inc(mixin_act, 1)

            act.wait_ge(mix_done, 1)
            unmix(nc.scalar.copy, 0)
            act.wait_ge(mix_done, 3)
            unmix(nc.scalar.copy, 2).then_inc(mixed_act, 1)

            def modes_step(n, u):
                if from_(n, 2):
                    act.wait_ge(t_done, n * 2 - 2)
                place_modes(nc.scalar.copy, (0, 1), n, u, modes_act)

            def cols_step(n, u):
                act.wait_ge(t_done, n * 2 + 1)
                nc.scalar.copy(cols[:, u, 0:6, :], ps[0:3 * NF, B_T, 0:6 * NW]).then_inc(cols_act, 1)

            def rows_step(n, u, it):
                if from_(it, 1):
                    act.wait_ge(out_done[u], it * 32)
                for k in (0, 2, 4):
                    act.wait_ge(f_done, n * 6 + k + 1)
                    place_rows(nc.scalar.copy, k, u).then_inc(
                        rows_act, PLACED[k] - (PLACED[k - 2] if k >= 2 else 0))

            act.wait_ge(turned, 1)
            modes_step(0, 0)
            modes_step(1, 1)
            cols_step(0, 0)
            act.wait_ge(turned, 2)
            for n in (1, 2):
                modes_step(n + 1, (n + 1) % 2)
                cols_step(n, n % 2)
                rows_step(n - 1, (n - 1) % 2, 0)
            with act.Fori(1, 3) as it:
                for u in (1, 0):
                    n = it * 2 + (2 - u)
                    modes_step(n + 1, 1 - u)
                    cols_step(n, u)
                    rows_step(n - 1, 1 - u, it)
            cols_step(N - 1, 1)
            for n in (N - 2, N - 1):
                rows_step(n, n % 2, n // 2)

        @block.vector
        def _(dve):
            tt, tr = nc.vector.tensor_tensor, nc.vector.tensor_reduce
            nc.vector.memset(idle[:, :], 0.5).then_inc(idle_ready, 1)
            dve.wait_ge(params_in, 32)
            dve.wait_ge(narrow_in, 16)
            par_g = [par[:, o:o + GROUPS] for o in (P_GAMMA, P_BETA, P_MEAN, P_VAR)]
            nc.vector.tensor_scalar(bn[:, 1, :], par_g[3], 1e-5, None, ALU.add).then_inc(setup, 1)
            nc.vector.scalar_tensor_tensor(gain[:, 0, :], par[:, P_IN:P_IN + C], 1.0, par[:, P_L:P_L + C],
                                           op0=ALU.add, op1=ALU.mult)
            tt(gain[:, 1, :], par[:, P_IN:P_IN + C], par[:, P_L:P_L + C], ALU.mult)
            nc.vector.tensor_scalar(gain[:, 2, :], par[:, P_H:P_H + C], 1.0, None, ALU.add).then_inc(setup, 1)
            dve.wait_ge(root_done, 1)
            nc.vector.reciprocal(lf[:, :], bn[:, 0, :]).then_inc(setup, 1)
            dve.wait_ge(setup, 3)

            def gains(i):
                return view(gain[:, i, 0:1], (0, J), (1, C))

            tt(bn[:, 0, :], par_g[0], lf[:, :], ALU.mult).then_inc(setup, 1)
            tt(view(kb_mul[:, 0:1], (C, J), (1, C)), gains(0),
               view(k_narrow[:, O_MA:O_MA + 1], (C, J), (1, C)), ALU.mult)
            tt(view(kb_add[:, 0:1], (C, J), (1, C)), gains(1),
               view(k_narrow[:, O_MC:O_MC + 1], (C, J), (1, C)), ALU.mult)
            tt(view(kb_tmp[:, 0:1], (C, J), (1, C)), gains(2),
               view(k_narrow[:, O_MB:O_MB + 1], (C, J), (1, C)), ALU.mult).then_inc(setup, 1)
            dve.wait_ge(setup, 5)
            tt(kb_add[:, :], kb_add[:, :], kb_tmp[:, :], ALU.add)
            tt(pick[:, :, :], view(bn[:, 0, 0:1], (1, GROUPS), (0, TAPS)),
               view(k_narrow[:, O_PICK:O_PICK + 1], (TAPS, GROUPS), (1, TAPS)), ALU.mult)
            tt(lf_bn[:, :], par_g[2], bn[:, 0, :], ALU.mult).then_inc(setup, 1)
            dve.wait_ge(setup, 6)
            tt(bn[:, 1, :], par_g[1], lf_bn[:, :], ALU.subtract).then_inc(setup, 1)
            dve.wait_ge(setup, 7)

            def taps(n):
                base = n * K_LINKS

                dve.wait_ge(lf_done, n + 1)
                tt(lf_all[:, :], ps[0:KROWS, B_LF, 0:GROUPS * TAPS],
                   view(pick[:, 0, 0:1], (1, GROUPS * TAPS)), ALU.mult).then_inc(k_step, 1)
                dve.wait_ge(k_step, base + 1)
                tr(lf[:, :], view(lf_all[:, 0:1], (TAPS, GROUPS), (1, TAPS)), AX.X, ALU.add).then_inc(k_step, 1)
                dve.wait_ge(k_step, base + 2)
                tt(lf_bn[:, :], lf[:, :], bn[:, 1, :], ALU.add).then_inc(bn_done, 1)
                dve.wait_ge(tanh_done, n + 1)
                tt(view(kb_tmp[:, 0:1], (C, J), (J, GROUPS), (1, C // GROUPS)),
                   view(lf_tanh[:, 0:1], (0, J), (1, GROUPS), (0, C // GROUPS)),
                   view(kb_mul[:, 0:1], (C, J), (J, GROUPS), (1, C // GROUPS)), ALU.mult).then_inc(k_step, 1)
                dve.wait_ge(k_step, base + 3)
                tt(kb[:, :], kb_tmp[:, :], kb_add[:, :], ALU.add).then_inc(kb_done, 1)

            def combine(m, u):
                base = m * F_LINKS
                entry = lambda at, *dims: view(data[:, u, at:at + 1], *dims)
                low = lambda at, *dims: view(ps[:, B_COEF, at:at + 1], *dims)
                edge = SQ * NU

                dve.wait_ge(coef_done, m + 1)
                dve.wait_ge(data_out, m + 1)
                tt(view(prod_a[:, 0, 0:1], (8 * SQ, 3), (8, SQ), (1, 4)), entry(2 * MODES, (0, 3), (NU, SQ), (1, 4)),
                   low(ND, (8 * SQ, 3), (8, SQ), (1, 4)), ALU.mult)
                tt(view(prod_a[:, 0, 4:5], (8, 3 * SQ), (1, 4)),
                   entry(edge + NEDGE // 2 - 1, (0, 3 * SQ), (NEDGE // 2, 4)),
                   low(ND + 4, (8, 3 * SQ), (1, 4)), ALU.mult).then_inc(f_step, 1)
                tt(view(terms[:, 0, 0:1], (MODES, SQ), (PLANE, 2), (1, MODES)),
                   entry(0, (NU, SQ), (MODES, 2), (1, MODES)),
                   low(0, (MODES, SQ), (PLANE, 2), (1, MODES)), ALU.mult)
                for s in range(S):
                    at = s * Q * MODES
                    last = tt(view(terms[:, 2, at:at + 1], (PLANE, 4), (MODES, Q), (1, MODES)),
                              entry(edge + s * MODES, (NEDGE // 2, 4), (0, Q), (1, MODES)),
                              view(ps[:, B_COEF + 1, at:at + 1], (PLANE, 4), (MODES, Q), (1, MODES)), ALU.mult)
                last.then_inc(coef_used, 1)
                dve.wait_ge(f_step, base + 1)
                tr(coef_a[:, :], prod_a[:, :, :], AX.X, ALU.add).then_inc(f_step, 1)
                dve.wait_ge(f_step, base + 2)
                tt(view(terms[:, 6, 0:1], (MODES, 3 * SQ), (1, MODES)), view(coef_a[:, 0:1], (1, 3 * SQ), (0, MODES)),
                   const(O_BAS, (MODES, 3 * SQ), (1, MODES)), ALU.mult).then_inc(f_step, 1)
                dve.wait_ge(f_step, base + 3)
                tr(xht[:, :], view(terms[:, 0, 0:1], (1, PLANE), (PLANE, NTERM)), AX.X, ALU.add).then_inc(f_step, 1)
                dve.wait_ge(f_step, base + 4)
                if from_(m, 2):
                    dve.wait_ge(acc_done, m - 1)
                half = Q * MODES
                tt(parts[:, u, 0, :], xht[:, 0:half], xht[:, half:], ALU.subtract).then_inc(f_step, 1)
                tt(parts[:, u, 1, :], xht[:, 0:half], xht[:, half:], ALU.add).then_inc(parts_done, 1)

            weight = [float(w) for w in gaussian()[REACH:]]

            def blur_weights(share):
                lo = w_raw[:, bass.ds(share * WSTEP, 1), REACH:REACH + 1]
                to = view(w_sb[:, bass.ds(share * WSTEP, 1), 0:1], (1, WSTEP * C))
                for k in range(1, REACH + 1):
                    dve.wait_ge(pairs_done, share * REACH + k)
                    if k > 1:
                        dve.wait_ge(blur_step, share * REACH + (k - 1))
                    nc.vector.scalar_tensor_tensor(
                        to if k == REACH else w_acc[:, :],
                        view(lo, (CPAD, WSTEP), (1, C)) if k == 1 else w_acc[:, :],
                        weight[k - 1] / weight[k],
                        view(w_pair[:, k - 1, 0, 0:1], (1, WSTEP * C)),
                        op0=ALU.mult, op1=ALU.add).then_inc(blur_step, 1)

            def load_step(m, u):
                combine(m, u)
                taps(m + 1)
                blur_weights(m)

            dve.wait_ge(rest_in, 16)
            taps(0)
            dve.wait_ge(weights_in, 16)
            for m in range(2):
                load_step(m, m)
            with dve.Fori(1, N // 2 - 1) as it:
                for u in range(2):
                    load_step(it * 2 + u, u)
            taps(N - 1)
            for m in (N - 2, N - 1):
                combine(m, m % 2)

            dve.wait_ge(acc_done, N - 1)
            dve.wait_ge(parts_done, N)
            dve.wait_ge(f_step, N * F_LINKS)
            share = blur_matrix(N)[:, N - 1]
            for k in np.flatnonzero(share):
                last = nc.vector.scalar_tensor_tensor(
                    acc[:, int(k), :], view(parts[:, 1, 0, 0:1], (1, PLANE)), float(share[k]), acc[:, int(k), :],
                    op0=ALU.mult, op1=ALU.add)
            last.then_inc(last_share, 1)
            dve.wait_ge(last_share, 1)
            dve.wait_ge(zeroed, 2)
            for j in range(J - 1):
                last = place_parts(nc.vector.tensor_copy, j)
            last.then_inc(mixin_dve, 1)

            dve.wait_ge(mix_done, 2)
            unmix(nc.vector.tensor_copy, 1).then_inc(mixed_dve, 1)
            dve.wait_ge(mixed_dve, 1)
            dve.wait_ge(mixed_act, 1)
            def turn(lo, hi):
                size = (hi - lo) * S * J * C
                nc.vector.transpose(view(mixed_t[0:Q * C, lo, 0:1], (1, size)),
                                    view(mixed[:, lo, 0, 0:1], (1, size))).then_inc(turned, 1)

            def modes_step(n, u):
                if from_(n, 2):
                    dve.wait_ge(t_done, n * 2 - 2)
                place_modes(nc.vector.tensor_copy, (2, 3), n, u, modes_dve)

            def cols_step(n, u):
                dve.wait_ge(t_done, n * 2 + 2)
                nc.vector.tensor_copy(cols[:, u, 6:TRIPLES, :],
                                      ps[0:3 * NF, B_T + 1, 0:(TRIPLES - 6) * NW]).then_inc(cols_dve, 1)

            def rows_step(n, u, it):
                if from_(it, 1):
                    dve.wait_ge(out_done[u], it * 32)
                for k in (1, 3, 5):
                    dve.wait_ge(f_done, n * 6 + k + 1)
                    place_rows(nc.vector.tensor_copy, k, u).then_inc(
                        rows_dve, PLACED[k] - (PLACED[k - 2] if k >= 2 else 0))

            turn(0, 2)
            dve.wait_ge(turned, 1)
            modes_step(0, 0)
            modes_step(1, 1)
            cols_step(0, 0)
            turn(2, N)
            dve.wait_ge(turned, 2)
            for n in (1, 2):
                modes_step(n + 1, (n + 1) % 2)
                cols_step(n, n % 2)
                rows_step(n - 1, (n - 1) % 2, 0)
            with dve.Fori(1, 3) as it:
                for u in (1, 0):
                    n = it * 2 + (2 - u)
                    modes_step(n + 1, 1 - u)
                    cols_step(n, u)
                    rows_step(n - 1, 1 - u, it)
            cols_step(N - 1, 1)
            for n in (N - 2, N - 1):
                rows_step(n, n % 2, n // 2)

        @block.gpsimd
        def _(pool):
            tt = nc.gpsimd.tensor_tensor
            nc.gpsimd.memset(mixin[:, :, :, :, :], 0.0)
            nc.gpsimd.memset(mixed[:, :, :, :], 0.0).then_inc(zeroed, 1)
            nc.gpsimd.memset(modes[:, :, :, :], 0.0)
            nc.gpsimd.memset(rows[:, :, :, :], 0.0).then_inc(zeroed, 1)
            pool.wait_ge(rest_in, 16)

            def spread_step(n, u):
                pool.wait_ge(parts_done, n + 1)
                pool.wait_ge(f_step, (n + 1) * F_LINKS)
                src = view(parts[:, u, 0, 0:1], (0, N), (1, PLANE))
                weight = view(k_wide[:, bass.ds(n * N + O_BT, 1)] if not isinstance(n, int) else
                              const(O_BT + n * N, (1, 1)), (1, N), (0, PLANE))
                if not from_(n, 1):
                    tt(acc[:, :, :], src, weight, ALU.mult).then_inc(acc_done, 1)
                    return
                pool.wait_ge(acc_done, n)
                tt(spread[:, :, :], src, weight, ALU.mult).then_inc(spread_done, 1)
                pool.wait_ge(spread_done, n)
                tt(acc[:, :, :], acc[:, :, :], spread[:, :, :], ALU.add).then_inc(acc_done, 1)

            def pair_step(share):
                for k in range(1, REACH + 1):
                    if from_(share, 1):
                        pool.wait_ge(blur_step, (share - 1) * REACH + k)
                    lo, hi = (view(w_raw[:, bass.ds(share * WSTEP, 1), REACH + d:REACH + d + 1], (CPAD, WSTEP), (1, C))
                              for d in (-k, k))
                    tt(w_pair[:, k - 1, :, :], lo, hi, ALU.add).then_inc(pairs_done, 1)

            pool.wait_ge(weights_in, 16)
            pair_step(0)
            spread_step(0, 0)
            pair_step(1)
            with pool.Fori(0, N // 2 - 2) as it:
                for m, u in ((it * 2 + 1, 1), (it * 2 + 2, 0)):
                    spread_step(m, u)
                    pair_step(m + 1)
            spread_step(N - 3, 1)
            spread_step(N - 2, 0)


def kernel(**inputs):
    import concourse.bacc as bacc
    from concourse.bass_utils import run_bass_kernel_spmd

    wide, narrow = constants()
    w1 = np.asarray(inputs["L1_conv_w1"])
    a_at = np.array([[[frequency(s, j, q) for q in range(Q)] for s in range(S)] for j in range(J)])
    b_at = np.array([[column(s, b) for b in range(MODES)] for s in range(S)])
    mix_w = w1[:, :, a_at[:, :, :, None], b_at[None, :, None, :]]
    mix_w = mix_w.transpose(2, 0, 3, 4, 5, 1).reshape(J * C, S * Q * MODES, C)
    edges = [0] * REACH + list(range(C)) + [C - 1] * REACH
    mix_w = np.ascontiguousarray(mix_w[:, :, edges])

    def per_channel(a):
        return np.broadcast_to(np.asarray(a).reshape(1, C), (KROWS, C))

    def per_tap(a):
        a = np.asarray(a).reshape(GROUPS, TAPS).T
        return np.repeat(np.concatenate([a, a[:1]], 0), J, axis=0)

    params = np.concatenate(
        [per_channel(inputs[f"L0_conv_{k}"]) for k in ("lamb_l", "lamb_h", "inside_all")]
        + [per_tap(inputs[f"L0_conv_bn_{k}"]) for k in ("gamma", "beta", "mean", "var")], 1)
    arrays = {
        "x": np.ascontiguousarray(inputs["x"]),
        "wide": wide,
        "narrow": narrow,
        "params": np.ascontiguousarray(params),
        "conv_wt": np.ascontiguousarray(np.asarray(inputs["L0_conv_conv_w"]).T),
        "mix_w": mix_w,
    }
    nc = bacc.Bacc("TRN2", target_bir_lowering=False, num_devices=1)
    args = [nc.dram_tensor(k, a.shape, mybir.dt.from_np(a.dtype), kind="ExternalInput").ap()
            for k, a in arrays.items()]
    out = nc.dram_tensor("out", (N, C, H, H), mybir.dt.float32, kind="ExternalOutput").ap()
    hartley_conv_kernel(nc, *args, out)
    result = run_bass_kernel_spmd(nc, [arrays], core_ids=[0])
    return result.results[0]["out"]
```

```python
from contextlib import ExitStack

import numpy as np

import concourse.bass as bass
from concourse import mybir

N, C, H = 8, 32, 128
MODES = 20
GROUPS, TAPS = 8, 9
J, Q, S = 4, 3, 2
SQ = S * Q
NP = SQ * 2 * J + 2 * J
NU = 2 * MODES + 4
NEDGE = 2 * (S * MODES + 1)
NDATA = SQ * NU + 2 * NEDGE
KT = TAPS + 1
KROWS = KT * J
PLANE = SQ * MODES
ND, NA, NB = 2 * PLANE, 3 * SQ * 8, 4 * PLANE
NTERM = 9
HALF = 33
NW = 2 * HALF
NF = MODES + 1
TRIPLES = 11
BPAD = 32
REACH = 4
CPAD = C + 2 * REACH
WSHARES = N - 2
WSTEP = S * Q * MODES // WSHARES

O_LT = 0
O_ID = 64
O_RU = O_ID + 128
O_RE = O_RU + S * 2 * NU
O_BAS = O_RE + NEDGE
O_BT = O_BAS + 3 * PLANE
O_TW = O_BT + N * N
O_LH = O_TW + NW
NC128 = O_LH + 3 * H
O_TAB = 0
O_MA = ND + NA + NB
O_MB, O_MC = O_MA + H, O_MA + 2 * H
O_PICK = O_MA + 3 * H
NC40 = O_PICK + GROUPS * TAPS
P_L, P_H, P_IN = 0, C, 2 * C
P_GAMMA = 3 * C
P_BETA, P_MEAN, P_VAR = P_GAMMA + GROUPS, P_GAMMA + 2 * GROUPS, P_GAMMA + 3 * GROUPS
NPAR = P_GAMMA + 4 * GROUPS


def frequency(s, j, q):
    a = min(Q * j + q, MODES // 2)
    return a if s == 0 else (MODES - a) % MODES


def column(s, b):
    return b if s == 0 else (MODES - b) % MODES


def gaussian():
    k = np.exp(-0.5 * np.arange(-REACH, REACH + 1, dtype=np.float32) ** 2)
    return (k / k.sum()).astype(np.float64)


def blur_matrix(n):
    k = gaussian()
    m = np.zeros((n, n))
    for o in range(n):
        for i in range(2 * REACH + 1):
            m[o, min(max(o + i - REACH, 0), n - 1)] += k[i]
    return m


def constants():
    th = 2 * np.pi / H
    h = np.arange(H)
    e1, e2 = np.zeros(H), np.zeros(H)
    e1[1], e1[H - 1] = 1, -1
    e2[H - 2], e2[0] = 1, -1
    lt = np.zeros((H, NP))
    ru = np.zeros((H, S, 2, NU))
    re = np.zeros((H, NEDGE))
    basis = np.zeros((3, S, Q, MODES))
    for s in range(S):
        for q in range(Q):
            for j in range(J):
                a = frequency(s, j, q)
                lt[:, ((s * Q + q) * 2) * J + j] = np.cos(th * a * h)
                lt[:, ((s * Q + q) * 2 + 1) * J + j] = np.sin(th * a * h)
        for b in range(MODES):
            bb = column(s, b)
            c, sn = np.cos(th * bb * h), np.sin(th * bb * h)
            ru[:, s, 0, b], ru[:, s, 0, MODES + b] = c, sn
            ru[:, s, 1, b], ru[:, s, 1, MODES + b] = -sn, c
            re[:, s * MODES + b], re[:, NEDGE // 2 + s * MODES + b] = c, sn
            basis[:, s, :, b] = np.array([1, np.cos(th * bb), np.sin(th * bb)])[:, None]
        ru[:, s, 0, 2 * MODES], ru[:, s, 0, 2 * MODES + 1] = e1, e2
        ru[:, s, 1, 2 * MODES + 2], ru[:, s, 1, 2 * MODES + 3] = e1, e2
    lt[:, NP - 2 * J:NP - J], lt[:, NP - J:] = e1[:, None], e2[:, None]
    re[:, NEDGE // 2 - 1], re[:, NEDGE - 1] = e1, e2

    d = np.zeros((KT, J, 2, S, Q, MODES))
    e = np.zeros((KT, J, 4, S, Q, MODES))
    f = np.zeros((KT, J, 3, S, Q, 8))
    for j in range(J):
        for s in range(S):
            for q in range(Q):
                a = frequency(s, j, q)
                ea = np.exp(1j * th * a)
                for b in range(MODES):
                    bb = column(s, b)
                    eb = np.exp(1j * th * bb)
                    g = 1 - 1j * np.conj(ea) * np.conj(eb)
                    for di in (-1, 0, 1):
                        for dj in (-1, 0, 1):
                            t = (di + 1) * 3 + dj + 1
                            k = g * ea ** di * eb ** dj
                            d[t, j, 0, s, q, b], d[t, j, 1, s, q, b] = k.real, k.imag
                            if di:
                                r = 0 if di < 0 else 2
                                z = g * (1 if di < 0 else ea) * eb ** dj
                                e[t, j, r, s, q, b], e[t, j, r + 1, s, q, b] = z.real, z.imag
                    if a == 0 and bb == 0:
                        d[TAPS, j, 0, s, q, b] = 1
                for di in (-1, 0, 1):
                    for dj in (-1, 1):
                        t, r = (di + 1) * 3 + dj + 1, (0 if dj < 0 else 1)
                        parts = [(r, ea ** di), (2 + r, -1j * ea ** di)]
                        if di:
                            parts.append((4 + (0 if di < 0 else 2) + r, 1 if di < 0 else ea))
                        for k, z in parts:
                            m = ([z, -1j * z * np.conj(ea), -z * np.conj(ea)] if dj < 0
                                 else [-1j * np.conj(ea) * z, z, 1j * z])
                            f[t, j, :, s, q, k] = np.real(m)
    table = np.concatenate([d.reshape(KROWS, ND), f.reshape(KROWS, NA), e.reshape(KROWS, NB)], 1)

    kept = np.concatenate([np.arange(HALF), np.arange(H - HALF, H)])
    tw = np.zeros((2, 2, BPAD, H))
    for b in range(MODES):
        tw[0, 0, b], tw[0, 1, b] = np.cos(th * h * b), -np.sin(th * h * (b + 1))
        tw[1, 0, b], tw[1, 1, b] = -np.sin(th * h * b), -np.cos(th * h * (b + 1))
    rows = blur_matrix(H)
    tw = (tw.reshape(128, H) @ rows.T)[:, kept] * (0.5 / (H * H) * gaussian()[-1])
    tw[:, HALF] = 0
    lh = np.zeros((3, 128, H))
    for s in range(3):
        for a in range(MODES + 1):
            lh[s, s * NF + a] = rows @ np.cos(th * h * a)
            lh[s, 64 + s * NF + a] = rows @ np.sin(th * h * a)

    wide = np.zeros((128, NC128), np.float32)
    wide[:, O_LT:O_LT + NP] = lt
    wide[:, O_ID:O_RU] = np.eye(128)
    wide[:, O_RU:O_RE] = ru.reshape(H, -1)
    wide[:, O_RE:O_BAS] = re
    wide[:, O_BAS:O_BT] = basis.reshape(1, -1)
    wide[:, O_BT:O_TW] = blur_matrix(N).T.reshape(1, -1)
    wide[:, O_TW:O_LH] = tw
    wide[:, O_LH:] = lh.transpose(1, 0, 2).reshape(128, -1)

    t, own = np.arange(KROWS) // J, np.kron(np.arange(KROWS) % J, 1)[:, None] == (np.arange(128) // C)[None]
    narrow = np.zeros((KROWS, NC40), np.float32)
    narrow[:, O_TAB:O_MA] = table
    narrow[:, O_MA:O_MB] = own * (t < TAPS)[:, None]
    narrow[:, O_MB:O_MC] = own * (t == TAPS // 2)[:, None]
    narrow[:, O_MC:O_PICK] = -1.0 * own * (t == TAPS)[:, None]
    narrow[:, O_PICK:] = np.tile(t[:, None] == np.arange(TAPS)[None], (1, GROUPS))
    return wide, narrow


def hartley_conv_kernel(nc, x, wide, narrow, params, conv_wt, mix_w, out):
    fp32 = mybir.dt.float32
    ALU = mybir.AluOpType
    ACT = mybir.ActivationFunctionType
    AX = mybir.AxisListType
    HC = C // 2
    G1 = 8
    NG1 = C // G1

    def view(ap, *dims):
        return bass.AP(tensor=ap.tensor, offset=ap.offset, ap=[ap.ap[0], *[list(d) for d in dims]])

    def from_(n, least):
        return not isinstance(n, int) or n >= least

    ctx = ExitStack()
    with ctx:
        def sb(name, shape):
            return ctx.enter_context(nc.sbuf_tensor(name, shape, fp32))

        def sem(name):
            return ctx.enter_context(nc.semaphore(name))

        x_ring = sb("x_ring", [H, 2, C * H])
        mixed_t = x_ring[:, 0].rearrange("p (n f) -> p n f", f=S * J * C)
        k_wide = sb("k_wide", [128, NC128])
        k_narrow = sb("k_narrow", [KROWS, NC40])
        par = sb("par", [KROWS, NPAR])
        conv_sb = sb("conv_sb", [C, GROUPS * TAPS])
        w_raw = sb("w_raw", [128, S * Q * MODES, CPAD])
        w_acc = sb("w_acc", [128, WSTEP * C])
        w_pair = sb("w_pair", [128, REACH, WSTEP, C])
        w_sb = sb("w_sb", [128, S * Q * MODES, C])
        freq = sb("freq", [128, 2, G1 // 2 * H])
        y_sb = sb("y_sb", [H, 2, NP, C])
        data = sb("data", [128, 2, NDATA])
        pooled = sb("pooled", [C, 1])
        bn = sb("bn", [KROWS, 2, GROUPS])
        gain = sb("gain", [KROWS, 3, C])
        pick = sb("pick", [KROWS, GROUPS, TAPS])
        kb_mul = sb("kb_mul", [KROWS, 128])
        kb_add = sb("kb_add", [KROWS, 128])
        kb_tmp = sb("kb_tmp", [KROWS, 128])
        kb = sb("kb", [KROWS, 128])
        lf_all = sb("lf_all", [KROWS, GROUPS * TAPS])
        lf = sb("lf", [KROWS, GROUPS])
        lf_bn = sb("lf_bn", [KROWS, GROUPS])
        lf_tanh = sb("lf_tanh", [KROWS, GROUPS])
        prod_a = sb("prod_a", [128, 3 * SQ, 8])
        coef_a = sb("coef_a", [128, 3 * SQ])
        terms = sb("terms", [128, NTERM, PLANE])
        xht = sb("xht", [128, PLANE])
        parts = sb("parts", [128, 2, 2, Q * MODES])
        spread = sb("spread", [128, N, PLANE])
        acc = sb("acc", [128, N, PLANE])
        idle = sb("idle", [128, 256])
        mixin = sb("mixin", [128, Q * MODES, J, 3, N])
        mixed = sb("mixed", [Q * C, N, S * J, BPAD])
        modes = sb("modes", [128, 2, (C + 1) * NF + 1])
        cols = sb("cols", [128, 2, TRIPLES, NW])
        rows = sb("rows", [H, 2, C, H])
        ps = ctx.enter_context(nc.psum_tensor("ps", [128, 8, 512], fp32))

        consts_in, params_in, narrow_in, rest_in = map(
            sem, ("consts_in", "params_in", "narrow_in", "rest_in"))
        weights_in = [sem(f"weights_in{i}") for i in range(2)]
        x_in = [sem(f"x_in{i}") for i in range(4)]
        x_first, idle_ready = sem("x_first"), sem("idle_ready")
        freq_out, turned_y = sem("freq_out"), sem("turned_y")
        s1_done, y_out, s2_first, s2_done, pool_done, data_out = map(
            sem, ("s1_done", "y_out", "s2_first", "s2_done", "pool_done", "data_out"))
        setup, root_done, lf_done, k_step, bn_done, tanh_done, kb_done = map(
            sem, ("setup", "root_done", "lf_done", "k_step", "bn_done", "tanh_done", "kb_done"))
        coef_done, coef_used, f_step, parts_done, spread_done, acc_done, last_share = map(
            sem, ("coef_done", "coef_used", "f_step", "parts_done", "spread_done", "acc_done", "last_share"))
        pairs_done, blur_step = map(sem, ("pairs_done", "blur_step"))
        zeroed, mixin_dve, mixin_act, mix_done, mixed_act, mixed_dve = map(
            sem, ("zeroed", "mixin_dve", "mixin_act", "mix_done", "mixed_act", "mixed_dve"))
        turned, modes_act, modes_dve, t_done, cols_act, cols_dve = map(
            sem, ("turned", "modes_act", "modes_dve", "t_done", "cols_act", "cols_dve"))
        f_done, rows_act, rows_dve = map(sem, ("f_done", "rows_act", "rows_dve"))
        out_first, out_done = sem("out_first"), [sem(f"out_done{i}") for i in range(2)]

        B_DATA, B_LF, B_COEF = 4, 5, 6
        B_T, B_F = 3, (5, 6, 7)
        K_LINKS, F_LINKS = 3, 5

        def const(offset, *dims):
            return view(k_wide[:, offset:offset + 1], *dims)

        block = ctx.enter_context(nc.Block())

        CHUNKS = [(s, t, (6 if t == 0 else (5 if s < 2 else 4))) for t in (0, 6) for s in range(3)]
        FIRST = 18
        PLACED = (1, 3, 3, 4, 5, 5)
        ROUND = 5

        def data_at(sq):
            if sq == 0:
                return ps[:, B_LF, GROUPS * TAPS:GROUPS * TAPS + NU]
            return ps[:, B_DATA, sq * NU:(sq + 1) * NU]

        @block.sync
        def _(sp):
            by_row = x.rearrange("n c h w -> n h c w")

            def load_images(n, u, lo, hi):
                return sp.dma_start(view(x_ring[:, u, lo * H:lo * H + 1], (H, hi - lo), (1, H)),
                                    by_row[n, :, lo:hi, :])

            def load(n, u, half):
                if from_(n, 2):
                    sp.wait_ge(s1_done, (n - 2) * NG1 + (half + 1) * NG1 // 2)
                load_images(n, u, half * HC, (half + 1) * HC).then_inc(x_in[2 * u + half], 16)

            sp.dma_start(k_wide[:, 0:O_BAS], wide[:, 0:O_BAS]).then_inc(consts_in, 16)
            load_images(0, 0, 0, G1).then_inc(x_first, 16)
            load_images(0, 0, G1, HC).then_inc(x_in[0], 16)
            load(0, 0, 1)
            load(1, 1, 0)
            sp.dma_start(par[:, :], params).then_inc(params_in, 16)
            sp.dma_start(conv_sb[:, :], conv_wt).then_inc(params_in, 16)
            sp.dma_start(k_narrow[:, :], narrow).then_inc(narrow_in, 16)
            load(1, 1, 1)
            sp.dma_start(k_wide[:, O_BAS:], wide[:, O_BAS:]).then_inc(rest_in, 16)
            part = S * Q * MODES // 2
            for n in range(2, N):
                for half in range(2):
                    load(n, n % 2, half)
                if n < 4:
                    cut = slice((n - 2) * part, (n - 1) * part)
                    sp.dma_start(w_raw[:, cut, :], mix_w[:, cut, :]).then_inc(weights_in[n - 2], 16)

            def store(n, u, lo, hi, placed):
                sp.wait_ge(rows_act, n * ROUND + placed)
                sp.wait_ge(rows_dve, n * ROUND + placed)
                dst = out[bass.ds(n, 1), lo:hi, :, :]
                sp.dma_start(dst.rearrange("a c h w -> h (a c) w"), rows[:, u, lo:hi, :]
                             ).then_inc(out_done[u], 16)

            for s in range(3):
                sp.wait_ge(rows_dve if s == 1 else rows_act, PLACED[s])
                sp.dma_start(out[0, s:FIRST:3, :, :].rearrange("c h w -> h c w"), rows[:, 0, s:FIRST:3, :]
                             ).then_inc(out_done[0] if s == 2 else out_first, 16)
            store(0, 0, FIRST, C, ROUND)
            store(1, 1, 0, FIRST, PLACED[1])
            store(1, 1, FIRST, C, ROUND)
            with sp.Fori(1, N // 2) as it:
                for u in range(2):
                    store(it * 2 + u, u, 0, FIRST, PLACED[1])
                    store(it * 2 + u, u, FIRST, C, ROUND)
            sp.wait_ge(out_first, 32)
            for u in range(2):
                sp.wait_ge(out_done[u], 32 * (N // 2))

        @block.tensor
        def _(pe):
            def keep_busy(count, bank=0):
                for _ in range(count):
                    nc.tensor.matmul(ps[:, bank, 0:256], idle[:, 0:128], idle[:, :], start=True, stop=True)

            def stage1(n, it, u, g):
                if isinstance(n, int) and n == 0 and g == 0:
                    pe.wait_ge(x_first, 16)
                elif g % 2 == 0 or (isinstance(n, int) and n == 0):
                    pe.wait_ge(x_in[2 * u + g // 2], it * 16 + 16)
                if from_(n, 1) or g >= 2:
                    pe.wait_ge(freq_out, n * NG1 + g - 1)
                for half in range(2):
                    at = (g * G1 + half * G1 // 2) * H
                    last = nc.tensor.matmul(ps[half * 64:half * 64 + 64, g % 2, :], const(O_LT, (1, 64)),
                                            x_ring[:, u, at:at + G1 // 2 * H], start=True, stop=True)
                last.then_inc(s1_done, 1)

            def turn_group(n, u, g):
                pe.wait_ge(freq_out, n * NG1 + g + 1)
                if from_(n, 1) or g >= 2:
                    pe.wait_ge(y_out, n * NG1 + g - 1)
                for i in range(G1 // 2):
                    last = nc.tensor.transpose(ps[:, 2 + g % 2, i * 128:(i + 1) * 128],
                                               freq[:, g % 2, i * H:(i + 1) * H], const(O_ID, (1, 128)))
                last.then_inc(turned_y, 1)

            def coefficients(m):
                pe.wait_ge(kb_done, m + 1)
                if from_(m, 1):
                    pe.wait_ge(coef_used, m)
                nc.tensor.matmul(ps[:, B_COEF, 0:ND + NA], kb[:, :], k_narrow[:, 0:ND + NA], start=True, stop=True)
                nc.tensor.matmul(ps[:, B_COEF + 1, 0:NB], kb[:, :], k_narrow[:, ND + NA:O_MA],
                                 start=True, stop=True).then_inc(coef_done, 1)

            def stage2(n, u, quarter):
                if quarter == 0:
                    pe.wait_ge(y_out, (n + 1) * NG1)
                    if from_(n, 1):
                        pe.wait_ge(data_out, n)
                if quarter < 3:
                    for sq in (2 * quarter, 2 * quarter + 1):
                        for cs in range(2):
                            last = nc.tensor.matmul(data_at(sq),
                                                    y_sb[:, u, (sq * 2 + cs) * J:(sq * 2 + cs + 1) * J, :],
                                                    const(O_RU + ((sq // Q) * 2 + cs) * NU, (1, NU)),
                                                    start=(cs == 0), stop=(cs == 1))
                        if sq == 0:
                            last.then_inc(s2_first, 1)
                else:
                    for r in range(2):
                        at = SQ * NU + r * NEDGE
                        last = nc.tensor.matmul(ps[:, B_DATA, at:at + NEDGE],
                                                y_sb[:, u, NP - 2 * J + r * J:NP - J + r * J, :],
                                                const(O_RE, (1, NEDGE)), start=True, stop=True)
                    last.then_inc(s2_done, 1)

            def filter_logits(n):
                if not from_(n, 1):
                    pe.wait_ge(params_in, 32)
                pe.wait_ge(pool_done, n + 1)
                if from_(n, 1):
                    pe.wait_ge(k_step, (n - 1) * K_LINKS + 1)
                nc.tensor.matmul(ps[0:KROWS, B_LF, 0:GROUPS * TAPS], view(pooled[:, 0:1], (0, KROWS)),
                                 conv_sb[:, :], start=True, stop=True).then_inc(lf_done, 1)

            def load_step(n, it, u):
                stage1(n, it, u, 0)
                stage2(n - 1, 1 - u, 0)
                stage1(n, it, u, 1)
                turn_group(n, u, 0)
                stage2(n - 1, 1 - u, 1)
                filter_logits(n - 1)
                stage1(n, it, u, 2)
                turn_group(n, u, 1)
                stage2(n - 1, 1 - u, 2)
                stage1(n, it, u, 3)
                turn_group(n, u, 2)
                stage2(n - 1, 1 - u, 3)
                coefficients(n - 1)
                turn_group(n, u, 3)

            pe.wait_ge(idle_ready, 1)
            keep_busy(3)
            pe.wait_ge(consts_in, 16)
            for g in range(NG1 + 1):
                if g < NG1:
                    stage1(0, 0, 0, g)
                if g > 0:
                    turn_group(0, 0, g - 1)
            load_step(1, 0, 1)
            with pe.Fori(1, N // 2) as it:
                for u in range(2):
                    load_step(it * 2 + u, it, u)
            keep_busy(2)
            stage2(N - 1, 1, 0)
            filter_logits(N - 1)
            for quarter in (1, 2, 3):
                stage2(N - 1, 1, quarter)
            coefficients(N - 1)
            keep_busy(8)

            pe.wait_ge(rest_in, 16)
            pe.wait_ge(parts_done, N)
            keep_busy(8)
            pe.wait_ge(blur_step, WSHARES * REACH)
            pe.wait_ge(mixin_dve, 1)
            pe.wait_ge(mixin_act, 1)
            for b in range(MODES):
                for q in range(Q):
                    at = (b % 8) * 2 * J * N
                    for s in range(S):
                        last = nc.tensor.matmul(
                            view(ps[q * C:(q + 1) * C, b // 8, at:at + 1], (1, 2 * J * N)),
                            w_sb[:, (s * Q + q) * MODES + b, :],
                            mixin[:, q * MODES + b, :, 1 - s:3 - s, :], start=(s == 0), stop=(s == 1))
                if b % 8 == 7 or b == MODES - 1:
                    last.then_inc(mix_done, 1)

            def await_modes(n):
                pe.wait_ge(modes_act, n + 1)
                pe.wait_ge(modes_dve, n + 1)
                if from_(n, 1):
                    pe.wait_ge(cols_act, n)
                    pe.wait_ge(cols_dve, n)

            def to_columns(n, u):
                for t in range(TRIPLES):
                    for half in (slice(0, 64), slice(64, 128)):
                        last = nc.tensor.matmul(ps[half, B_T + t // 6, (t % 6) * NW:(t % 6 + 1) * NW],
                                                modes[half, u, 3 * t * NF:3 * t * NF + 64],
                                                k_wide[half, O_TW:O_TW + NW], start=True, stop=True)
                    if t in (5, TRIPLES - 1):
                        last.then_inc(t_done, 1)

            def to_rows(n, u, part, next_columns=False):
                if part == 0:
                    pe.wait_ge(cols_act, n + 1)
                else:
                    pe.wait_ge(cols_dve, n + 1)
                for k in range(3 * part, 3 * part + 3):
                    s, t, nt = CHUNKS[k]
                    if k >= 3:
                        pe.wait_ge(rows_dve if k % 2 == 0 else rows_act, n * ROUND + PLACED[k - 3])
                    elif from_(n, 1):
                        pe.wait_ge(rows_dve if k % 2 == 0 else rows_act, (n - 1) * ROUND + PLACED[k + 3])
                    if k == 2 and next_columns:
                        await_modes(n + 1)
                    nc.tensor.matmul(ps[:, B_F[k % 3], 0:nt * NW],
                                     const(O_LH + s * H, (1, H)), cols[:, u, t:t + nt, :],
                                     start=True, stop=True).then_inc(f_done, 1)

            keep_busy(2, B_COEF + 1)
            pe.wait_ge(mixed_dve, 1)
            pe.wait_ge(mixed_act, 1)
            keep_busy(6, B_COEF + 1)
            await_modes(0)
            to_columns(0, 0)

            def write_step(n, u):
                to_rows(n, u, 0, next_columns=True)
                to_columns(n + 1, 1 - u)
                to_rows(n, u, 1)

            write_step(0, 0)
            with pe.Fori(0, N // 2 - 1) as it:
                for n, u in ((it * 2 + 1, 1), (it * 2 + 2, 0)):
                    write_step(n, u)
            to_rows(N - 1, 1, 0)
            to_rows(N - 1, 1, 1)

        def slot_view(n, part, sj, count):
            at = mixed_t[part, bass.ds(n, 1), sj * C:sj * C + 1]
            return view(at, (C, count), (1, C))

        def place_modes(copy, quadrants, n, u):
            for quad in quadrants:
                v = quad % 2
                part = slice(32 * quad, 32 * quad + 32)
                for q in range(Q):
                    rows_q = slice(q * C, q * C + C)
                    for s in range(S):
                        js = [j for j in range(J) if (Q * j + q <= MODES // 2 if s == 0
                                                      else 0 < Q * j + q < MODES // 2)]
                        c = Q * js[0] + q
                        at = (c if s == 0 else MODES - c) + v
                        step = Q if s == 0 else -Q
                        last = copy(view(modes[part, u, at:at + 1], (step, len(js)), (NF, C)),
                                    slot_view(n, rows_q, s * J + js[0], len(js)))
            return last

        def place_rows(copy, k, u):
            s, t, nt = CHUNKS[k]
            return copy(view(rows[:, u, 3 * t + s, 0:1], (3 * H, nt), (H - HALF, 2), (1, HALF)),
                        view(ps[:, B_F[k % 3], 0:1], (NW, nt), (HALF, 2), (1, HALF)))

        def unmix(copy, bank):
            b0, nb = bank * 8, min(8, MODES - bank * 8)
            copy(view(mixed[:, 0, 0, b0:b0 + 1], (BPAD, J), (S * J * BPAD, N), (1, nb)),
                 view(ps[0:Q * C, bank, 0:1], (2 * N, J), (1, N), (2 * J * N, nb)))
            skip = 0
            if bank == 0:
                skip = 1
                copy(view(mixed[:, 0, J, 0:1], (BPAD, J), (S * J * BPAD, N)),
                     view(ps[0:Q * C, 0, N:N + 1], (2 * N, J), (1, N)))
            first, at = MODES - b0 - skip, N + skip * 2 * J * N
            return copy(view(mixed[:, 0, J, first:first + 1], (BPAD, J), (S * J * BPAD, N), (-1, nb - skip)),
                        view(ps[0:Q * C, bank, at:at + 1], (2 * N, J), (1, N), (2 * J * N, nb - skip)))

        def place_parts(copy, j):
            part = slice(C * j, C * j + C)
            return copy(view(mixin[part, 0, j, 0, 0:1], (N, 2), (J * 3 * N, Q * MODES), (1, N)),
                        view(acc[part, 0, 0:1], (Q * MODES, 2), (1, Q * MODES), (PLANE, N)))

        def place_minus_odd(j):
            part = slice(C * j, C * j + C)
            return nc.scalar.mul(view(mixin[part, 0, j, 2, 0:1], (J * 3 * N, Q * MODES), (1, N)),
                                 view(acc[part, 0, 0:1], (1, Q * MODES), (PLANE, N)), -1.0)

        @block.scalar
        def _(act):
            def keep_freq(n, g):
                act.wait_ge(s1_done, n * NG1 + g + 1)
                nc.scalar.copy(freq[:, g % 2, :], ps[:, g % 2, :]).then_inc(freq_out, 1)

            def keep_y(n, u, g):
                act.wait_ge(turned_y, n * NG1 + g + 1)
                nc.scalar.copy(view(y_sb[:, u, 0, g * G1:g * G1 + 1], (1, G1 // 2), (G1 // 2, 2), (C, NP)),
                               view(ps[:, 2 + g % 2, 0:1], (128, G1 // 2), (64, 2), (1, NP))).then_inc(y_out, 1)

            def keep_sums(m, u):
                act.wait_ge(s2_first, m + 1)
                nc.scalar.copy(data[:, u, 0:NU], data_at(0))
                nc.scalar.mul(pooled[:, :], ps[0:C, B_LF, GROUPS * TAPS:GROUPS * TAPS + 1], 1.0 / (H * H)
                              ).then_inc(pool_done, 1)

            def tanh(m):
                act.wait_ge(bn_done, m + 1)
                nc.scalar.activation(lf_tanh[:, :], lf_bn[:, :], ACT.Tanh).then_inc(tanh_done, 1)

            def keep_data(m, u):
                act.wait_ge(s2_done, m + 1)
                nc.scalar.copy(data[:, u, NU:], ps[:, B_DATA, NU:NDATA]).then_inc(data_out, 1)

            def load_step(n, u):
                keep_freq(n, 0)
                keep_sums(n - 1, 1 - u)
                keep_freq(n, 1)
                keep_y(n, u, 0)
                keep_freq(n, 2)
                tanh(n - 1)
                keep_y(n, u, 1)
                keep_freq(n, 3)
                keep_y(n, u, 2)
                keep_data(n - 1, 1 - u)
                keep_y(n, u, 3)

            for g in range(NG1 + 1):
                if g < NG1:
                    keep_freq(0, g)
                if g > 0:
                    keep_y(0, 0, g - 1)
            act.wait_ge(setup, 1)
            nc.scalar.activation(bn[:, 0, :], bn[:, 1, :], ACT.Sqrt).then_inc(root_done, 1)
            load_step(1, 1)
            with act.Fori(1, N // 2) as it:
                for u in range(2):
                    load_step(it * 2 + u, u)
            keep_sums(N - 1, 1)
            tanh(N - 1)
            keep_data(N - 1, 1)

            act.wait_ge(last_share, 1)
            act.wait_ge(zeroed, 2)
            for j in range(J):
                last = place_minus_odd(j)
            last.then_inc(mixin_act, 1)

            act.wait_ge(mix_done, 1)
            unmix(nc.scalar.copy, 0)
            act.wait_ge(mix_done, 3)
            unmix(nc.scalar.copy, 2).then_inc(mixed_act, 1)

            def modes_step(n, u, k):
                if from_(n, 2) and k == 0:
                    act.wait_ge(t_done, n * 2 - 2)
                last = place_modes(nc.scalar.copy, (k,), n, u)
                if k == 1:
                    last.then_inc(modes_act, 1)

            def cols_step(n, u):
                act.wait_ge(t_done, n * 2 + 1)
                nc.scalar.copy(cols[:, u, 0:6, :], ps[:, B_T, 0:6 * NW]).then_inc(cols_act, 1)

            def rows_step(n, u, it, chunks):
                if from_(it, 1) and chunks[0] < 3:
                    act.wait_ge(out_done[u], it * 32)
                for k in chunks:
                    act.wait_ge(f_done, n * 6 + k + 1)
                    place_rows(nc.scalar.copy, k, u).then_inc(
                        rows_act, PLACED[k] - (PLACED[k - 2] if k >= 2 else 0))

            def write_step(n, u, it):
                rows_step(n, u, it, (0, 2))
                modes_step(n + 2, u, 0)
                cols_step(n + 1, 1 - u)
                rows_step(n, u, it, (4,))
                modes_step(n + 2, u, 1)

            act.wait_ge(turned, 1)
            modes_step(0, 0, 0)
            modes_step(0, 0, 1)
            act.wait_ge(turned, 2)
            modes_step(1, 1, 0)
            cols_step(0, 0)
            modes_step(1, 1, 1)
            for n in (0, 1):
                write_step(n, n, 0)
            act.wait_ge(turned, 3)
            act.wait_ge(out_first, 32)
            with act.Fori(1, N // 2 - 1) as it:
                for u in range(2):
                    write_step(it * 2 + u, u, it)
            rows_step(N - 2, 0, N // 2 - 1, (0, 2))
            cols_step(N - 1, 1)
            rows_step(N - 2, 0, N // 2 - 1, (4,))
            rows_step(N - 1, 1, N // 2 - 1, (0, 2, 4))

        @block.vector
        def _(dve):
            tt, tr = nc.vector.tensor_tensor, nc.vector.tensor_reduce
            nc.vector.memset(idle[:, :], 0.5).then_inc(idle_ready, 1)
            dve.wait_ge(params_in, 32)
            dve.wait_ge(narrow_in, 16)
            par_g = [par[:, o:o + GROUPS] for o in (P_GAMMA, P_BETA, P_MEAN, P_VAR)]
            nc.vector.tensor_scalar(bn[:, 1, :], par_g[3], 1e-5, None, ALU.add).then_inc(setup, 1)
            nc.vector.scalar_tensor_tensor(gain[:, 0, :], par[:, P_IN:P_IN + C], 1.0, par[:, P_L:P_L + C],
                                           op0=ALU.add, op1=ALU.mult)
            tt(gain[:, 1, :], par[:, P_IN:P_IN + C], par[:, P_L:P_L + C], ALU.mult)
            nc.vector.tensor_scalar(gain[:, 2, :], par[:, P_H:P_H + C], 1.0, None, ALU.add).then_inc(setup, 1)
            dve.wait_ge(root_done, 1)
            nc.vector.reciprocal(lf[:, :], bn[:, 0, :]).then_inc(setup, 1)
            dve.wait_ge(setup, 3)

            def gains(i):
                return view(gain[:, i, 0:1], (0, J), (1, C))

            tt(bn[:, 0, :], par_g[0], lf[:, :], ALU.mult).then_inc(setup, 1)
            tt(view(kb_mul[:, 0:1], (C, J), (1, C)), gains(0),
               view(k_narrow[:, O_MA:O_MA + 1], (C, J), (1, C)), ALU.mult)
            tt(view(kb_add[:, 0:1], (C, J), (1, C)), gains(1),
               view(k_narrow[:, O_MC:O_MC + 1], (C, J), (1, C)), ALU.mult)
            tt(view(kb_tmp[:, 0:1], (C, J), (1, C)), gains(2),
               view(k_narrow[:, O_MB:O_MB + 1], (C, J), (1, C)), ALU.mult).then_inc(setup, 1)
            dve.wait_ge(setup, 5)
            tt(kb_add[:, :], kb_add[:, :], kb_tmp[:, :], ALU.add)
            tt(pick[:, :, :], view(bn[:, 0, 0:1], (1, GROUPS), (0, TAPS)),
               view(k_narrow[:, O_PICK:O_PICK + 1], (TAPS, GROUPS), (1, TAPS)), ALU.mult)
            tt(lf_bn[:, :], par_g[2], bn[:, 0, :], ALU.mult).then_inc(setup, 1)
            dve.wait_ge(setup, 6)
            tt(bn[:, 1, :], par_g[1], lf_bn[:, :], ALU.subtract).then_inc(setup, 1)
            dve.wait_ge(setup, 7)

            def taps(n):
                base = n * K_LINKS

                dve.wait_ge(lf_done, n + 1)
                tt(lf_all[:, :], ps[0:KROWS, B_LF, 0:GROUPS * TAPS],
                   view(pick[:, 0, 0:1], (1, GROUPS * TAPS)), ALU.mult).then_inc(k_step, 1)
                dve.wait_ge(k_step, base + 1)
                tr(lf[:, :], view(lf_all[:, 0:1], (TAPS, GROUPS), (1, TAPS)), AX.X, ALU.add).then_inc(k_step, 1)
                dve.wait_ge(k_step, base + 2)
                tt(lf_bn[:, :], lf[:, :], bn[:, 1, :], ALU.add).then_inc(bn_done, 1)
                dve.wait_ge(tanh_done, n + 1)
                tt(view(kb_tmp[:, 0:1], (C, J), (J, GROUPS), (1, C // GROUPS)),
                   view(lf_tanh[:, 0:1], (0, J), (1, GROUPS), (0, C // GROUPS)),
                   view(kb_mul[:, 0:1], (C, J), (J, GROUPS), (1, C // GROUPS)), ALU.mult).then_inc(k_step, 1)
                dve.wait_ge(k_step, base + 3)
                tt(kb[:, :], kb_tmp[:, :], kb_add[:, :], ALU.add).then_inc(kb_done, 1)

            def combine_products(m, u):
                entry = lambda at, *dims: view(data[:, u, at:at + 1], *dims)
                low = lambda at, *dims: view(ps[:, B_COEF, at:at + 1], *dims)
                edge = SQ * NU

                dve.wait_ge(coef_done, m + 1)
                dve.wait_ge(data_out, m + 1)
                tt(view(prod_a[:, 0, 0:1], (8 * SQ, 3), (8, SQ), (1, 4)), entry(2 * MODES, (0, 3), (NU, SQ), (1, 4)),
                   low(ND, (8 * SQ, 3), (8, SQ), (1, 4)), ALU.mult)
                tt(view(prod_a[:, 0, 4:5], (8, 3 * SQ), (1, 4)),
                   entry(edge + NEDGE // 2 - 1, (0, 3 * SQ), (NEDGE // 2, 4)),
                   low(ND + 4, (8, 3 * SQ), (1, 4)), ALU.mult).then_inc(f_step, 1)
                tt(view(terms[:, 0, 0:1], (MODES, SQ), (PLANE, 2), (1, MODES)),
                   entry(0, (NU, SQ), (MODES, 2), (1, MODES)),
                   low(0, (MODES, SQ), (PLANE, 2), (1, MODES)), ALU.mult)
                for s in range(S):
                    at = s * Q * MODES
                    last = tt(view(terms[:, 2, at:at + 1], (PLANE, 4), (MODES, Q), (1, MODES)),
                              entry(edge + s * MODES, (NEDGE // 2, 4), (0, Q), (1, MODES)),
                              view(ps[:, B_COEF + 1, at:at + 1], (PLANE, 4), (MODES, Q), (1, MODES)), ALU.mult)
                last.then_inc(coef_used, 1)

            def combine_sum(m, u):
                base = m * F_LINKS
                dve.wait_ge(f_step, base + 1)
                tr(coef_a[:, :], prod_a[:, :, :], AX.X, ALU.add).then_inc(f_step, 1)
                dve.wait_ge(f_step, base + 2)
                tt(view(terms[:, 6, 0:1], (MODES, 3 * SQ), (1, MODES)), view(coef_a[:, 0:1], (1, 3 * SQ), (0, MODES)),
                   const(O_BAS, (MODES, 3 * SQ), (1, MODES)), ALU.mult).then_inc(f_step, 1)
                dve.wait_ge(f_step, base + 3)
                dve.wait_ge(coef_used, m + 1)
                tr(xht[:, :], view(terms[:, 0, 0:1], (1, PLANE), (PLANE, NTERM)), AX.X, ALU.add).then_inc(f_step, 1)
                dve.wait_ge(f_step, base + 4)
                if from_(m, 2):
                    dve.wait_ge(acc_done, m - 1)
                half = Q * MODES
                tt(parts[:, u, 0, :], xht[:, 0:half], xht[:, half:], ALU.subtract).then_inc(f_step, 1)
                tt(parts[:, u, 1, :], xht[:, 0:half], xht[:, half:], ALU.add).then_inc(parts_done, 1)

            weight = [float(w) for w in gaussian()[REACH:]]

            def blur_weights(share):
                lo = w_raw[:, bass.ds(share * WSTEP, 1), REACH:REACH + 1]
                to = view(w_sb[:, bass.ds(share * WSTEP, 1), 0:1], (1, WSTEP * C))
                for k in range(1, REACH + 1):
                    dve.wait_ge(pairs_done, share * REACH + k)
                    if k > 1:
                        dve.wait_ge(blur_step, share * REACH + (k - 1))
                    nc.vector.scalar_tensor_tensor(
                        to if k == REACH else w_acc[:, :],
                        view(lo, (CPAD, WSTEP), (1, C)) if k == 1 else w_acc[:, :],
                        weight[k - 1] / weight[k],
                        view(w_pair[:, k - 1, 0, 0:1], (1, WSTEP * C)),
                        op0=ALU.mult, op1=ALU.add).then_inc(blur_step, 1)

            def load_step(m, u):
                combine_products(m, u)
                combine_sum(m, u)
                taps(m + 1)
                blur_weights(m)

            dve.wait_ge(rest_in, 16)
            taps(0)
            dve.wait_ge(weights_in[0], 16)
            for m in range(2):
                load_step(m, m)
            dve.wait_ge(weights_in[1], 16)
            with dve.Fori(1, N // 2 - 1) as it:
                for u in range(2):
                    load_step(it * 2 + u, u)
            combine_products(N - 2, 0)
            taps(N - 1)
            combine_sum(N - 2, 0)
            combine_products(N - 1, 1)
            combine_sum(N - 1, 1)

            dve.wait_ge(acc_done, N - 1)
            dve.wait_ge(parts_done, N)
            dve.wait_ge(f_step, N * F_LINKS)
            share = blur_matrix(N)[:, N - 1]
            for k in np.flatnonzero(share):
                last = nc.vector.scalar_tensor_tensor(
                    acc[:, int(k), :], view(parts[:, 1, 0, 0:1], (1, PLANE)), float(share[k]), acc[:, int(k), :],
                    op0=ALU.mult, op1=ALU.add)
            last.then_inc(last_share, 1)
            dve.wait_ge(last_share, 1)
            dve.wait_ge(zeroed, 2)
            for j in range(J):
                last = place_parts(nc.vector.tensor_copy, j)
            last.then_inc(mixin_dve, 1)

            dve.wait_ge(mix_done, 2)
            unmix(nc.vector.tensor_copy, 1).then_inc(mixed_dve, 1)
            dve.wait_ge(mixed_dve, 1)
            dve.wait_ge(mixed_act, 1)
            def turn(lo, hi):
                size = (hi - lo) * S * J * C
                nc.vector.transpose(view(mixed_t[0:Q * C, lo, 0:1], (1, size)),
                                    view(mixed[:, lo, 0, 0:1], (1, size))).then_inc(turned, 1)

            def modes_step(n, u, k):
                if from_(n, 2) and k == 0:
                    dve.wait_ge(t_done, n * 2 - 2)
                last = place_modes(nc.vector.tensor_copy, (2 + k,), n, u)
                if k == 1:
                    last.then_inc(modes_dve, 1)

            def cols_step(n, u):
                dve.wait_ge(t_done, n * 2 + 2)
                nc.vector.tensor_copy(cols[:, u, 6:TRIPLES, :],
                                      ps[:, B_T + 1, 0:(TRIPLES - 6) * NW]).then_inc(cols_dve, 1)

            def rows_step(n, u, it, chunks):
                if from_(it, 1) and chunks[0] < 3:
                    dve.wait_ge(out_done[u], it * 32)
                for k in chunks:
                    dve.wait_ge(f_done, n * 6 + k + 1)
                    place_rows(nc.vector.tensor_copy, k, u).then_inc(
                        rows_dve, PLACED[k] - (PLACED[k - 2] if k >= 2 else 0))

            def write_step(n, u, it):
                rows_step(n, u, it, (1,))
                modes_step(n + 2, u, 0)
                cols_step(n + 1, 1 - u)
                rows_step(n, u, it, (3, 5))
                modes_step(n + 2, u, 1)

            turn(0, 1)
            dve.wait_ge(turned, 1)
            modes_step(0, 0, 0)
            modes_step(0, 0, 1)
            turn(1, 4)
            dve.wait_ge(turned, 2)
            modes_step(1, 1, 0)
            cols_step(0, 0)
            modes_step(1, 1, 1)
            write_step(0, 0, 0)
            turn(4, N)
            write_step(1, 1, 0)
            dve.wait_ge(turned, 3)
            dve.wait_ge(out_first, 32)
            with dve.Fori(1, N // 2 - 1) as it:
                for u in range(2):
                    write_step(it * 2 + u, u, it)
            rows_step(N - 2, 0, N // 2 - 1, (1,))
            cols_step(N - 1, 1)
            rows_step(N - 2, 0, N // 2 - 1, (3, 5))
            rows_step(N - 1, 1, N // 2 - 1, (1, 3, 5))

        @block.gpsimd
        def _(pool):
            tt = nc.gpsimd.tensor_tensor
            nc.gpsimd.memset(mixin[:, :, :, :, :], 0.0)
            nc.gpsimd.memset(mixed[:, :, :, :], 0.0).then_inc(zeroed, 1)
            nc.gpsimd.memset(modes[:, :, :], 0.0)
            nc.gpsimd.memset(rows[:, :, :, :], 0.0).then_inc(zeroed, 1)
            pool.wait_ge(rest_in, 16)

            def spread_step(n, u):
                pool.wait_ge(parts_done, n + 1)
                pool.wait_ge(f_step, (n + 1) * F_LINKS)
                lo = max(n - REACH, 0) if isinstance(n, int) else 0
                src = view(parts[:, u, 0, 0:1], (0, N - lo), (1, PLANE))
                weight = view(k_wide[:, bass.ds(n * N + (O_BT + lo), 1)], (1, N - lo), (0, PLANE))
                if not from_(n, 1):
                    tt(acc[:, :, :], src, weight, ALU.mult).then_inc(acc_done, 1)
                    return
                pool.wait_ge(acc_done, n)
                tt(spread[:, lo:, :], src, weight, ALU.mult).then_inc(spread_done, 1)
                pool.wait_ge(spread_done, n)
                tt(acc[:, lo:, :], acc[:, lo:, :], spread[:, lo:, :], ALU.add).then_inc(acc_done, 1)

            def pair_step(share):
                for k in range(1, REACH + 1):
                    if from_(share, 1):
                        pool.wait_ge(blur_step, (share - 1) * REACH + k)
                    lo, hi = (view(w_raw[:, bass.ds(share * WSTEP, 1), REACH + d:REACH + d + 1], (CPAD, WSTEP), (1, C))
                              for d in (-k, k))
                    tt(w_pair[:, k - 1, :, :], lo, hi, ALU.add).then_inc(pairs_done, 1)

            pool.wait_ge(weights_in[0], 16)
            pair_step(0)
            spread_step(0, 0)
            pair_step(1)
            pool.wait_ge(weights_in[1], 16)
            with pool.Fori(0, N // 2 - 2) as it:
                for m, u in ((it * 2 + 1, 1), (it * 2 + 2, 0)):
                    spread_step(m, u)
                    pair_step(m + 1)
            spread_step(N - 3, 1)
            spread_step(N - 2, 0)


def kernel(**inputs):
    import concourse.bacc as bacc
    from concourse.bass_utils import run_bass_kernel_spmd

    wide, narrow = constants()
    w1 = np.asarray(inputs["L1_conv_w1"])
    a_at = np.array([[[frequency(s, j, q) for q in range(Q)] for s in range(S)] for j in range(J)])
    b_at = np.array([[column(s, b) for b in range(MODES)] for s in range(S)])
    mix_w = w1[:, :, a_at[:, :, :, None], b_at[None, :, None, :]]
    mix_w = mix_w.transpose(2, 0, 3, 4, 5, 1).reshape(J * C, S * Q * MODES, C)
    edges = [0] * REACH + list(range(C)) + [C - 1] * REACH
    mix_w = np.ascontiguousarray(mix_w[:, :, edges])

    def per_channel(a):
        return np.broadcast_to(np.asarray(a).reshape(1, C), (KROWS, C))

    def per_tap(a):
        a = np.asarray(a).reshape(GROUPS, TAPS).T
        return np.repeat(np.concatenate([a, a[:1]], 0), J, axis=0)

    params = np.concatenate(
        [per_channel(inputs[f"L0_conv_{k}"]) for k in ("lamb_l", "lamb_h", "inside_all")]
        + [per_tap(inputs[f"L0_conv_bn_{k}"]) for k in ("gamma", "beta", "mean", "var")], 1)
    arrays = {
        "x": np.ascontiguousarray(inputs["x"]),
        "wide": wide,
        "narrow": narrow,
        "params": np.ascontiguousarray(params),
        "conv_wt": np.ascontiguousarray(np.asarray(inputs["L0_conv_conv_w"]).T),
        "mix_w": mix_w,
    }
    nc = bacc.Bacc("TRN2", target_bir_lowering=False, num_devices=1)
    args = [nc.dram_tensor(k, a.shape, mybir.dt.from_np(a.dtype), kind="ExternalInput").ap()
            for k, a in arrays.items()]
    out = nc.dram_tensor("out", (N, C, H, H), mybir.dt.float32, kind="ExternalOutput").ap()
    hartley_conv_kernel(nc, *args, out)
    result = run_bass_kernel_spmd(nc, [arrays], core_ids=[0])
    return result.results[0]["out"]
```
